# Optimizing a Trainium2 kernel written in Bass

```python
import numpy as np
import jax
import jax.numpy as jnp

def _softmax(x, axis=-1):
    return jax.nn.softmax(x, axis=axis)

def _gelu(x):
    return jax.nn.gelu(x, approximate=True)

def _silu(x):
    return jax.nn.silu(x)

def _sigmoid(x):
    return jax.nn.sigmoid(x)

def _layernorm(x, axis=-1, eps=1e-05):
    m = jnp.mean(x, axis=axis, keepdims=True)
    v = jnp.var(x, axis=axis, keepdims=True)
    return (x - m) / jnp.sqrt(v + eps)

def _scatter_add(tgt, idx, src, axis=0):
    return tgt.at[idx].add(src)

def _segment_sum(src, seg, n):
    return jax.ops.segment_sum(src, seg, n)
kernel_name = 'mk_gnn_preln_d4_gnn_r32_b95f37'

def setup_inputs(seed: int=0):
    np.random.seed(seed)
    _w = jnp.asarray

    def _rec_inputs():
        import jax
        import jax.numpy as jnp
        _gk = jax.random.key(seed)
        x = -0.0002117 + 1 * jax.random.normal(jax.random.fold_in(_gk, 1), (3125, 256), jnp.float32)
        src = jax.random.randint(jax.random.fold_in(_gk, 2), (50000,), 0, 3125, jnp.int32)
        dst = jnp.minimum((3125 * jax.random.uniform(jax.random.fold_in(_gk, 3), (50000,)) ** 2.0).astype(jnp.int32), 99999)
        _o = jnp.argsort(dst, stable=True)
        src = src[_o]
        dst = dst[_o]
        edge_type_16 = jax.random.randint(jax.random.fold_in(_gk, 13), (50000,), 0, 16, jnp.int32)
        return (x, src, dst, edge_type_16)
    x, src, dst, edge_type_16 = _rec_inputs()

    def _L0_gnn_setup():
        import jax, jax.numpy as jnp
        import numpy as np
        N_NODES = 3125
        F_DIM = 256
        NNZ = 50000

        def _prelu(x, a):
            return jnp.where(x >= 0, x, a * x)

        def _hconv(x, W, b, src, dst, n):
            xt = x @ W
            ones = jnp.ones(src.shape, xt.dtype)
            D = jax.ops.segment_sum(ones, src, num_segments=n)
            B = jax.ops.segment_sum(ones, dst, num_segments=n)
            Dinv = jnp.where(D > 0, 1.0 / D, 0.0)
            Binv = jnp.where(B > 0, 1.0 / B, 0.0)
            m = jax.ops.segment_sum(xt[src], dst, num_segments=n) * Binv[:, None]
            out = jax.ops.segment_sum(m[dst], src, num_segments=n) * Dinv[:, None]
            return out + b
        key = jax.random.key(seed)
        k0, k1, k2, k3 = jax.random.split(key, 4)
        x = jax.random.normal(k0, (N_NODES, F_DIM), dtype=jnp.float32)
        edge_index = jax.random.randint(k1, (2, NNZ), 0, N_NODES, dtype=jnp.int32)
        scale = (2.0 / F_DIM) ** 0.5
        W1 = jax.random.normal(k2, (F_DIM, F_DIM), dtype=jnp.float32) * scale
        W2 = jax.random.normal(k3, (F_DIM, F_DIM), dtype=jnp.float32) * scale
        b1 = jnp.zeros((F_DIM,), jnp.float32)
        b2 = jnp.zeros((F_DIM,), jnp.float32)
        a = jnp.full((1,), 0.25, jnp.float32)
        return {'x': x, 'edge_index': edge_index, 'W1': W1, 'b1': b1, 'W2': W2, 'b2': b2, 'a': a}
    _L0_gnn_all = _L0_gnn_setup()
    _L0_gnn_in = {k: v for k, v in _L0_gnn_all.items() if k in ('W1', 'b1', 'W2', 'b2', 'a')}
    del _L0_gnn_all

    def _L1_gnn_setup():
        import jax, jax.numpy as jnp
        import numpy as np
        N_NODES = 50000
        N_EDGES = 25000
        HDIM = 256
        NUMRELS = 16

        def _gru_cell(x, h, w_ih, w_hh, b_ih, b_hh):
            gi = x @ w_ih.T + b_ih
            gh = h @ w_hh.T + b_hh
            i_r, i_z, i_n = jnp.split(gi, 3, axis=-1)
            h_r, h_z, h_n = jnp.split(gh, 3, axis=-1)
            r = jax.nn.sigmoid(i_r + h_r)
            z = jax.nn.sigmoid(i_z + h_z)
            n = jnp.tanh(i_n + r * h_n)
            return (1.0 - z) * n + z * h
        key = jax.random.key(seed)
        ks = jax.random.split(key, 9)
        h = jax.random.normal(ks[0], (N_NODES, HDIM), dtype=jnp.float32)
        relvectors = jax.random.normal(ks[1], (NUMRELS, HDIM), dtype=jnp.float32)
        s = 1.0 / np.sqrt(HDIM)
        w_ih = jax.random.uniform(ks[2], (3 * HDIM, HDIM), minval=-s, maxval=s, dtype=jnp.float32)
        w_hh = jax.random.uniform(ks[3], (3 * HDIM, HDIM), minval=-s, maxval=s, dtype=jnp.float32)
        b_ih = jax.random.uniform(ks[4], (3 * HDIM,), minval=-s, maxval=s, dtype=jnp.float32)
        b_hh = jax.random.uniform(ks[5], (3 * HDIM,), minval=-s, maxval=s, dtype=jnp.float32)
        edge_src = jax.random.randint(ks[6], (N_EDGES,), 0, N_NODES, dtype=jnp.int32)
        edge_dst = jax.random.randint(ks[7], (N_EDGES,), 0, N_NODES, dtype=jnp.int32)
        edge_rel = jax.random.randint(ks[8], (N_EDGES,), 0, NUMRELS, dtype=jnp.int32)
        return {'h': h, 'relvectors': relvectors, 'w_ih': w_ih, 'w_hh': w_hh, 'b_ih': b_ih, 'b_hh': b_hh, 'edge_src': edge_src, 'edge_dst': edge_dst, 'edge_rel': edge_rel}
    _L1_gnn_all = _L1_gnn_setup()
    _L1_gnn_in = {k: v for k, v in _L1_gnn_all.items() if k in ('relvectors', 'w_ih', 'w_hh', 'b_ih', 'b_hh')}
    del _L1_gnn_all

    def _L2_gnn_setup():
        import jax, jax.numpy as jnp
        import numpy as np
        N_NODES = 50000
        N_EDGES = 312500
        WIDTH = 256
        LN_EPS = 1e-05

        def gcn_conv(x, edge_index, W, b):
            n = x.shape[0]
            loops = jnp.arange(n, dtype=edge_index.dtype)
            src = jnp.concatenate([edge_index[0], loops])
            dst = jnp.concatenate([edge_index[1], loops])
            deg = jax.ops.segment_sum(jnp.ones_like(dst, dtype=x.dtype), dst, num_segments=n)
            dinv = jnp.where(deg > 0, jax.lax.rsqrt(deg), 0.0)
            norm = dinv[src] * dinv[dst]
            h = x @ W.T
            msgs = norm[:, None] * h[src]
            out = jax.ops.segment_sum(msgs, dst, num_segments=n)
            return out + b

        def layer_norm(x, gamma, beta):
            mu = jnp.mean(x, axis=-1, keepdims=True)
            var = jnp.mean(jnp.square(x - mu), axis=-1, keepdims=True)
            return (x - mu) * jax.lax.rsqrt(var + LN_EPS) * gamma + beta
        key = jax.random.key(seed)
        k1, k2, k3, k4 = jax.random.split(key, 4)
        x = jax.random.normal(k1, (N_NODES, WIDTH), dtype=jnp.float32)
        edge_index = jax.random.randint(k2, (2, N_EDGES), 0, N_NODES, dtype=jnp.int64)
        W = jax.random.normal(k3, (WIDTH, WIDTH), dtype=jnp.float32) / np.sqrt(WIDTH)
        b = jax.random.normal(k4, (WIDTH,), dtype=jnp.float32) * 0.01
        gamma = jnp.ones((WIDTH,), dtype=jnp.float32)
        beta = jnp.zeros((WIDTH,), dtype=jnp.float32)
        return {'x': x, 'edge_index': edge_index, 'W': W, 'b': b, 'gamma': gamma, 'beta': beta}
    _L2_gnn_all = _L2_gnn_setup()
    _L2_gnn_in = {k: v for k, v in _L2_gnn_all.items() if k in ('W', 'b', 'gamma', 'beta')}
    del _L2_gnn_all

    def _L3_gnn_setup():
        import jax, jax.numpy as jnp
        import numpy as np
        N, IN_CH, HEADS, OUT_CH, E = (50000, 256, 4, 64, 25000)
        key = jax.random.key(seed)
        k1, k2, k3, k4, k5 = jax.random.split(key, 5)
        x = jax.random.normal(k1, (N, IN_CH), dtype=jnp.float32)
        edge_index = jax.random.randint(k2, (2, E), 0, N, dtype=jnp.int64)
        bw = float(np.sqrt(6.0 / (IN_CH + HEADS * OUT_CH)))
        ba = float(np.sqrt(6.0 / (HEADS + OUT_CH)))
        weight = jax.random.uniform(k3, (IN_CH, HEADS * OUT_CH), jnp.float32, -bw, bw)
        attn_l = jax.random.uniform(k4, (HEADS, OUT_CH), jnp.float32, -ba, ba)
        attn_r = jax.random.uniform(k5, (HEADS, OUT_CH), jnp.float32, -ba, ba)
        return {'x': x, 'edge_index': edge_index, 'weight': weight, 'attn_l': attn_l, 'attn_r': attn_r}
    _L3_gnn_all = _L3_gnn_setup()
    _L3_gnn_in = {k: v for k, v in _L3_gnn_all.items() if k in ('weight', 'attn_l', 'attn_r')}
    del _L3_gnn_all
    return {'x': x, 'src': src, 'dst': dst, 'edge_type_16': edge_type_16, 'L0_gnn_W1': _L0_gnn_in['W1'], 'L0_gnn_b1': _L0_gnn_in['b1'], 'L0_gnn_W2': _L0_gnn_in['W2'], 'L0_gnn_b2': _L0_gnn_in['b2'], 'L0_gnn_a': _L0_gnn_in['a'], 'L1_gnn_relvectors': _L1_gnn_in['relvectors'], 'L1_gnn_w_ih': _L1_gnn_in['w_ih'], 'L1_gnn_w_hh': _L1_gnn_in['w_hh'], 'L1_gnn_b_ih': _L1_gnn_in['b_ih'], 'L1_gnn_b_hh': _L1_gnn_in['b_hh'], 'L2_gnn_W': _L2_gnn_in['W'], 'L2_gnn_b': _L2_gnn_in['b'], 'L2_gnn_gamma': _L2_gnn_in['gamma'], 'L2_gnn_beta': _L2_gnn_in['beta'], 'L3_gnn_weight': _L3_gnn_in['weight'], 'L3_gnn_attn_l': _L3_gnn_in['attn_l'], 'L3_gnn_attn_r': _L3_gnn_in['attn_r']}

def reference(x, src, dst, edge_type_16, L0_gnn_W1, L0_gnn_b1, L0_gnn_W2, L0_gnn_b2, L0_gnn_a, L1_gnn_relvectors, L1_gnn_w_ih, L1_gnn_w_hh, L1_gnn_b_ih, L1_gnn_b_hh, L2_gnn_W, L2_gnn_b, L2_gnn_gamma, L2_gnn_beta, L3_gnn_weight, L3_gnn_attn_l, L3_gnn_attn_r):
    import jax
    import jax.numpy as jnp

    def _L0_gnn_ref(x, edge_index, W1, b1, W2, b2, a):
        import jax, jax.numpy as jnp
        import numpy as np
        N_NODES = 3125
        F_DIM = 256
        NNZ = 50000

        def _prelu(x, a):
            return jnp.where(x >= 0, x, a * x)

        def _hconv(x, W, b, src, dst, n):
            xt = x @ W
            ones = jnp.ones(src.shape, xt.dtype)
            D = jax.ops.segment_sum(ones, src, num_segments=n)
            B = jax.ops.segment_sum(ones, dst, num_segments=n)
            Dinv = jnp.where(D > 0, 1.0 / D, 0.0)
            Binv = jnp.where(B > 0, 1.0 / B, 0.0)
            m = jax.ops.segment_sum(xt[src], dst, num_segments=n) * Binv[:, None]
            out = jax.ops.segment_sum(m[dst], src, num_segments=n) * Dinv[:, None]
            return out + b
        src, dst = (edge_index[0], edge_index[1])
        n = x.shape[0]
        h = _prelu(_hconv(x, W1, b1, src, dst, n), a)
        h = _hconv(h, W2, b2, src, dst, n) + x
        return _prelu(h, a)

    def _L1_gnn_ref(h, relvectors, w_ih, w_hh, b_ih, b_hh, edge_src, edge_dst, edge_rel):
        import jax, jax.numpy as jnp
        import numpy as np
        N_NODES = 50000
        N_EDGES = 25000
        HDIM = 256
        NUMRELS = 16

        def _gru_cell(x, h, w_ih, w_hh, b_ih, b_hh):
            gi = x @ w_ih.T + b_ih
            gh = h @ w_hh.T + b_hh
            i_r, i_z, i_n = jnp.split(gi, 3, axis=-1)
            h_r, h_z, h_n = jnp.split(gh, 3, axis=-1)
            r = jax.nn.sigmoid(i_r + h_r)
            z = jax.nn.sigmoid(i_z + h_z)
            n = jnp.tanh(i_n + r * h_n)
            return (1.0 - z) * n + z * h
        msg = h[edge_src] + relvectors[edge_rel]
        red = jax.ops.segment_sum(msg, edge_dst, num_segments=h.shape[0])
        return _gru_cell(red, h, w_ih, w_hh, b_ih, b_hh)

    def _L2_gnn_ref(x, edge_index, W, b, gamma, beta):
        import jax, jax.numpy as jnp
        import numpy as np
        N_NODES = 50000
        N_EDGES = 312500
        WIDTH = 256
        LN_EPS = 1e-05

        def gcn_conv(x, edge_index, W, b):
            n = x.shape[0]
            loops = jnp.arange(n, dtype=edge_index.dtype)
            src = jnp.concatenate([edge_index[0], loops])
            dst = jnp.concatenate([edge_index[1], loops])
            deg = jax.ops.segment_sum(jnp.ones_like(dst, dtype=x.dtype), dst, num_segments=n)
            dinv = jnp.where(deg > 0, jax.lax.rsqrt(deg), 0.0)
            norm = dinv[src] * dinv[dst]
            h = x @ W.T
            msgs = norm[:, None] * h[src]
            out = jax.ops.segment_sum(msgs, dst, num_segments=n)
            return out + b

        def layer_norm(x, gamma, beta):
            mu = jnp.mean(x, axis=-1, keepdims=True)
            var = jnp.mean(jnp.square(x - mu), axis=-1, keepdims=True)
            return (x - mu) * jax.lax.rsqrt(var + LN_EPS) * gamma + beta
        h = gcn_conv(x, edge_index, W, b)
        h = layer_norm(h, gamma, beta)
        h = jax.nn.relu(h)
        return h

    def _L3_gnn_ref(x, edge_index, weight, attn_l, attn_r):
        import jax, jax.numpy as jnp
        import numpy as np
        N, IN_CH, HEADS, OUT_CH, E = (50000, 256, 4, 64, 25000)
        heads, out_ch = attn_l.shape
        n = x.shape[0]
        xt = jnp.matmul(x, weight).reshape(-1, heads, out_ch)
        row, col = (edge_index[0], edge_index[1])
        alpha_l = jnp.einsum('ehd,hd->eh', xt[row], attn_l)
        alpha_r = jnp.einsum('ehd,hd->eh', xt[col], attn_r)
        alpha = jax.nn.softmax(jax.nn.leaky_relu(alpha_l + alpha_r, 0.01), axis=1)
        tmp = jnp.einsum('nh,nhd->nd', alpha[:n], xt[col[:n]])
        out = jnp.broadcast_to(tmp[:, None, :], (n, heads, out_ch))
        return out.reshape(n, heads * out_ch)
    edge_index = jnp.stack([src, dst])
    h = jnp.maximum(_layernorm(x, axis=-1), 0.0)
    x = x + _L0_gnn_ref(h, edge_index, L0_gnn_W1, L0_gnn_b1, L0_gnn_W2, L0_gnn_b2, L0_gnn_a)
    h = jnp.maximum(_layernorm(x, axis=-1), 0.0)
    x = x + _L1_gnn_ref(h, L1_gnn_relvectors, L1_gnn_w_ih, L1_gnn_w_hh, L1_gnn_b_ih, L1_gnn_b_hh, src, dst, edge_type_16)
    h = jnp.maximum(_layernorm(x, axis=-1), 0.0)
    x = x + _L2_gnn_ref(h, edge_index, L2_gnn_W, L2_gnn_b, L2_gnn_gamma, L2_gnn_beta)
    h = jnp.maximum(_layernorm(x, axis=-1), 0.0)
    x = x + _L3_gnn_ref(h, edge_index, L3_gnn_weight, L3_gnn_attn_l, L3_gnn_attn_r)
    return x

_drawn_inputs = setup_inputs


def setup_inputs(seed=0):
    import zlib

    import numpy as np

    out = dict(_drawn_inputs(seed))
    spreads = {'L0_gnn_b1': (0.0, 0.1),
     'L0_gnn_b2': (0.0, 0.1),
     'L2_gnn_gamma': (1.0, 0.2),
     'L2_gnn_beta': (0.0, 0.1)}
    factors = {'L1_gnn_b_ih': 8.0, 'L1_gnn_b_hh': 8.0, 'L2_gnn_b': 8.0}
    for name, (base, spread) in spreads.items():
        noise = np.random.default_rng([zlib.crc32(name.encode()), seed]).standard_normal(out[name].shape)
        drawn = base * np.exp(spread * noise) if base else spread * noise
        out[name] = jnp.asarray(drawn.astype(out[name].dtype))
    for name, factor in factors.items():
        out[name] = (out[name] * factor).astype(out[name].dtype)
    return out
```

```python
from contextlib import ExitStack

import concourse.bass as bass
from concourse import mybir

F32, BF16, F16 = mybir.dt.float32, mybir.dt.bfloat16, mybir.dt.float16
F8, I32, U32 = mybir.dt.float8e4, mybir.dt.int32, mybir.dt.uint32
ALU = mybir.AluOpType
ACT = mybir.ActivationFunctionType
AX = mybir.AxisListType

NODES, EDGES, FEAT, RELS, HEADS = 3125, 50000, 256, 16, 4
P = 125
TILES = NODES // P
CHUNKS = EDGES // P
PITCH = 128
ROW = TILES * PITCH
WORDS = PITCH // 4
WIN = 25
WPT = P // WIN
WINDOWS = NODES // WIN
KEYS = TILES * WIN
HALF_A = 13
SLOTS = 4
KW = 640
DH = FEAT // HEADS
KC = FEAT // 128
ZW = FEAT + 2 * HEADS
UP = 2048.0
CNT = 8.0
EPS = 1e-5


def pipelined(eng, stages):
    lag = max(l for l, _ in stages)
    first = (lag + 3) // 2 * 2

    def step(k, half, par):
        for l, fn in stages:
            if isinstance(k, int) and not 0 <= k - l < TILES:
                continue
            fn(k - l, (par - l) % 2, half + (par - l) // 2)

    for k in range(first):
        step(k, k // 2, k % 2)
    with eng.Fori(first // 2, TILES // 2) as r:
        step(2 * r, r, 0)
        step(2 * r + 1, r, 1)
    for k in range(TILES - 1, TILES + lag):
        step(k, k // 2, k % 2)


def wait_past(eng, sem, value):
    if not (isinstance(value, int) and value <= 0):
        eng.wait_ge(sem, value)


def settle(eng, k):
    eng.sem_inc(k.noted, 1)


class Chain:

    def __init__(self, eng, sem, per_tile):
        self.eng, self.sem, self.per_tile, self.n = eng, sem, per_tile, 0

    def tile(self, i):
        assert self.n in (0, self.per_tile)
        self.base, self.n = i * self.per_tile, 0
        return self

    def link(self, ins):
        self.n += 1
        assert self.n <= self.per_tile
        ins.then_inc(self.sem, 1)
        self.eng.wait_ge(self.sem, self.base + self.n)
        return self


class Kernel:

    def __init__(self, nc, ctx, d):
        self.nc, self.ctx, self.d = nc, ctx, d
        self.phase_sems = []
        self.noted = nc.alloc_semaphore(name="noted")
        sb = self.sb
        self.ps = ctx.enter_context(nc.psum_tensor("ps", [128, 8, 512], F32))
        self.adj = sb("adj", [P, TILES, ROW], F8)
        self.pairA = sb("pairA", [P, TILES, 2 * FEAT], F16)
        self.pairB = sb("pairB", [P, TILES, 2 * FEAT], F16)
        self.blk = [sb(f"blk{i}", [P, ROW], F8) for i in range(2)]
        self.row = [sb(f"row{i}", [P, ROW], F8) for i in range(2)]
        self.xin = [sb(f"xin{i}", [P, FEAT], F32) for i in range(2)]
        self.ho = [sb(f"ho{i}", [P, FEAT], F32) for i in range(2)]
        self.work = sb("work", [128, 8 * FEAT + 2 * 2 * KC * P], F32)
        tile = [self.work[0:P, FEAT * n:FEAT * (n + 1)] for n in range(8)]
        self.hin, self.aw, self.t, self.xo = tile[0:2], tile[2:4], tile[4:6], tile[6:8]
        self.tT = [self.work[:, 8 * FEAT + n * 2 * KC * P:8 * FEAT + (n + 1) * 2 * KC * P]
                   .rearrange("f (c p) -> f c p", p=P) for n in range(2)]
        self.st = [sb(f"st{i}", [P, 16], F32) for i in range(2)]
        self.W1 = sb("W1", [128, KC, FEAT], F32)
        self.W2 = sb("W2", [128, KC, FEAT], F32)
        self.wih = sb("wih", [128, KC, 3 * FEAT], F32)
        self.whh = sb("whh", [128, KC, 3 * FEAT], F32)
        self.Wg = sb("Wg", [128, KC, FEAT], F32)
        self.Wz = sb("Wz", [128, KC, ZW], F32)
        self.b1 = sb("b1", [P, FEAT], F32)
        self.b2 = sb("b2", [P, FEAT], F32)
        self.bg = sb("bg", [P, FEAT], F32)
        self.gamma = sb("gamma", [P, FEAT], F32)
        self.beta = sb("beta", [P, FEAT], F32)
        self.bi = sb("bi", [P, 3 * FEAT], F32)
        self.bhn = sb("bhn", [P, FEAT], F32)
        self.rel = sb("rel", [RELS, FEAT], F32)
        self.ident = sb("ident", [P, 128], F32)
        self.identb = sb("identb", [P, 128], BF16)
        self.ones = sb("ones", [128, P], F32)
        self.mhalf = sb("mhalf", [P, 32], F32)
        self.slope = sb("slope", [P, 1], F32)
        self.gslope = sb("gslope", [P, 1], F32)
        self.gscale = sb("gscale", [P, 1], F32)
        self.gunscale = sb("gunscale", [P, 1], F32)
        self.CT = sb("CT", [RELS, TILES, P], F32)
        self.indeg = sb("indeg", [P, 32], F32)
        self.odeg8 = sb("odeg8", [P, 32], F32)
        self.rsB = sb("rsB", [P, 32], F32)
        self.rsD = sb("rsD", [P, 32], F32)
        self.rsD4 = sb("rsD4", [P, 32], F32)
        self.dinv = sb("dinv", [P, 32], F32)
        self.dinvs = sb("dinvs", [P, 32], F32)
        self.dinvu = sb("dinvu", [P, 32], F32)
        self.st2 = [sb(f"st2{i}", [P, 12], F32) for i in range(2)]
        self.st_i = sb("st_i", [P, 2, TILES], I32)
        self.al = sb("al", [P, TILES, HEADS], F32)
        self.table = sb("table", [1, 3 * 128], I32)
        self.flag = sb("flag", [1, 1], I32)
        self.extra = [sb(f"extra{i}", [P, FEAT], F32) for i in range(2)]
        self.junk = self.whh[0:P, :, :].rearrange("f c n -> f (c n)")[:, 0:ROW // 4].bitcast(F8)
        rows_f = [r[:, :].bitcast(F32) for r in self.row]
        self.rz, self.tmp = rows_f[0][:, 0:2 * FEAT], rows_f[0][:, 2 * FEAT:3 * FEAT]
        self.new, self.sum = rows_f[1][:, 0:FEAT], rows_f[1][:, FEAT:2 * FEAT]
        self.z = [rows_f[0][:, 0:ZW], rows_f[1][:, 2 * FEAT:2 * FEAT + ZW]]
        self.total = rows_f[0][:, 0:5 * DH]
        self.x3 = self.pairA[:, :, :].bitcast(F32)
        flat = self.pairB[:, :, :].rearrange("p t f -> p (t f)")
        self.oh_din = flat[:, 0:CHUNKS * WIN].bitcast(BF16)
        keys = flat[:, CHUNKS * WIN:CHUNKS * WIN + 6 * CHUNKS].bitcast(F32)
        self.lo_key, self.rel_key, self.hi_key = (keys[:, CHUNKS * n:CHUNKS * (n + 1)] for n in range(3))
        self.iota_keys = self.row[1][:, 0:2 * KW].bitcast(F16)
        self.iota_lo = self.row[1][:, 2 * KW:2 * KW + 512].bitcast(F32)
        self.win_off = self.row[1][:, 2 * KW + 512:2 * KW + 1024].bitcast(F32)
        ring = self.work[0:P, 0:SLOTS * (KW + 128 + 16) // 2].bitcast(BF16)
        self.oh_keys = ring[:, 0:SLOTS * KW]
        self.oh_lo = ring[:, SLOTS * KW:SLOTS * (KW + 128)]
        self.oh_rel = ring[:, SLOTS * (KW + 128):SLOTS * (KW + 144)]
        self.over = self.row[0][:, :].bitcast(U32)

    def sb(self, name, shape, dt):
        return self.ctx.enter_context(self.nc.sbuf_tensor(name, shape, dt))

    def sem(self, name):
        self.phase_sems.append(self.nc.alloc_semaphore(name=name))
        return self.phase_sems[-1]

    def end_phase(self):
        for s in self.phase_sems:
            self.nc.sync.sem_clear(s)
            self.nc.release_semaphore(s)
        self.phase_sems = []
        self.nc.all_engine_barrier()

    def sems(self, name):
        return [self.sem(name + "0"), self.sem(name + "1")]


def rows(ap, i):
    return ap[bass.ds(i * P, P), :]


def either(eng, k, run):
    general = eng.value_load(k.flag[0:1, 0:1], min_val=0, max_val=1)
    with eng.If(general > 0):
        run(True)
    with eng.Else():
        run(False)


def edge_sums(k, name, x, key, other, value, outdegree=False):
    nc, d = k.nc, k.d
    DEEP = 4
    loaded, gathered = ([k.sem(f"{name}_{n}{m}") for m in range(DEEP)] for n in ("indexed", "gathered"))
    made, hot, summed, out_ready, stored, ok = (k.sem(f"{name}_{n}") for n in (
        "made", "hot", "summed", "out", "stored", "ok"))
    iota, offset, zero = k.work[0:P, 0:128], k.work[0:P, 128:160], k.work[0:P, 256:512]
    ends = [k.work[0:P, 160 + 2 * n:162 + 2 * n].bitcast(I32) for n in range(DEEP)]
    keyf = [k.work[0:P, 160 + 2 * DEEP + n:161 + 2 * DEEP + n] for n in range(DEEP)]
    xg = [k.work[0:P, 512 + FEAT * n:512 + FEAT * (n + 1)] for n in range(DEEP)]
    oh = [k.work[0:P, 512 + DEEP * FEAT + 128 * n:512 + DEEP * FEAT + 128 * n + P] for n in range(DEEP)]

    with nc.Block() as block:

        @block.sync
        def _(sp):
            def run(general):
                if not general:
                    return
                with sp.Fori(0, TILES) as i:
                    with sp.Fori(0, CHUNKS // DEEP) as h:
                        for slot in range(DEEP):
                            c = DEEP * h + slot
                            sp.wait_ge(summed, CHUNKS * i + c + 1)
                            settle(sp, k)
                            sp.dma_start(ends[slot][:, 0:1], d[key][:, bass.ds(c, 1)], allow_slow_non_contiguous=True).then_inc(loaded[slot], 16)
                            sp.dma_start(ends[slot][:, 1:2], d[other][:, bass.ds(c, 1)], allow_slow_non_contiguous=True).then_inc(loaded[slot], 16)
                    sp.wait_ge(out_ready, i + 2)
                    settle(sp, k)
                    sp.dma_start(rows(d["extra"], i), k.extra[0][:, :]).then_inc(stored, 16)
                sp.wait_ge(stored, 16 * TILES + 1)

            either(sp, k, run)

        @block.gpsimd
        def _(pool):
            def run(general):
                if not general:
                    return
                g = nc.gpsimd
                g.iota(iota, pattern=[[1, 128]], base=0, channel_multiplier=0, allow_small_or_imprecise_dtypes=True)
                g.iota(offset, pattern=[[-P, 32]], base=0, channel_multiplier=0, allow_small_or_imprecise_dtypes=True)
                g.memset(zero, 0.0).then_inc(made, 1)
                with pool.Fori(0, TILES * CHUNKS // DEEP) as h:
                    for slot in range(DEEP):
                        pool.wait_ge(loaded[slot], 32 * h + 32)
                        settle(pool, k)
                        g.indirect_dma_start(xg[slot], None, x[:, :], bass.IndirectOffsetOnAxis(ap=ends[slot][:, 1:2], axis=0)
                                             ).then_inc(gathered[slot], 16)

            either(pool, k, run)

        @block.vector
        def _(dve):
            def run(general):
                if not general:
                    return
                v = nc.vector
                dve.wait_ge(made, 1)
                with dve.Fori(0, TILES) as i:
                    with dve.Fori(0, CHUNKS // DEEP) as h:
                        for slot in range(DEEP):
                            dve.wait_ge(loaded[slot], 32 * (CHUNKS // DEEP * i + h + 1))
                            v.tensor_copy(keyf[slot], ends[slot][:, 0:1]).then_inc(ok, 1)
                            dve.wait_ge(ok, CHUNKS * i + DEEP * h + slot + 1)
                            settle(dve, k)
                            v.tensor_scalar(oh[slot], iota[:, 0:P], keyf[slot], offset[:, bass.ds(i, 1)],
                                            ALU.subtract, ALU.is_equal).then_inc(hot, 1)

            either(dve, k, run)

        @block.tensor
        def _(pe):
            def run(general):
                if not general:
                    return
                pe.wait_ge(made, 1)
                pe.sem_inc(summed, DEEP)
                with pe.Fori(0, TILES) as i:
                    pe.wait_ge(out_ready, i + 1)
                    pe.matmul(k.ps[0:P, 7, 0:FEAT], zero[:, 0:P], zero, start=True, stop=True, skip_group_check=True)
                    if outdegree:
                        pe.matmul(k.ps[0:P, 6, 0:1], zero[:, 0:P], k.ones[0:P, 0:1], start=True, stop=True,
                                  skip_group_check=True)
                    with pe.Fori(0, CHUNKS // DEEP) as h:
                        for slot in range(DEEP):
                            pe.wait_ge(gathered[slot], 16 * (CHUNKS // DEEP * i + h + 1))
                            pe.wait_ge(hot, CHUNKS * i + DEEP * h + slot + 1)
                            if outdegree:
                                pe.matmul(k.ps[0:P, 6, 0:1], oh[slot], k.ones[0:P, 0:1], start=False, stop=True,
                                          skip_group_check=True)
                            pe.matmul(k.ps[0:P, 7, 0:FEAT], oh[slot], xg[slot], start=False, stop=True,
                                      skip_group_check=True).then_inc(summed, 1)

            either(pe, k, run)

        @block.scalar
        def _(act):
            def run(general):
                if not general:
                    return
                act.sem_inc(stored, 1)
                act.sem_inc(out_ready, 1)
                with act.Fori(0, TILES) as i:
                    act.wait_ge(summed, CHUNKS * i + CHUNKS + DEEP)
                    act.wait_ge(stored, 16 * i + 1)
                    settle(act, k)
                    if outdegree:
                        nc.scalar.activation(k.odeg8[:, bass.ds(i, 1)], k.ps[0:P, 6, 0:1], ACT.Copy, scale=1.0 / CNT)
                    nc.scalar.activation(k.extra[0][:, :], k.ps[0:P, 7, 0:FEAT], ACT.Copy,
                                         scale=value).then_inc(out_ready, 1)

            either(act, k, run)


def setup(k):
    nc, d = k.nc, k.d
    loaded, edges, made, ok = k.sem("setup_loaded"), k.sem("setup_edges"), k.sem("setup_made"), k.sem("setup_ok")
    picked, turned, bound = k.sem("setup_picked"), k.sem("setup_turned"), k.sem("setup_bound")
    have_pick, have_count, have_abs = k.sem("setup_have_pick"), k.sem("setup_have_count"), k.sem("setup_have_abs")
    flat = k.pairA[:, :, :].rearrange("p t f -> p (t f)").bitcast(F32)
    part = [flat[:, CHUNKS * n:CHUNKS * (n + 1)] for n in range(12)]
    raw = flat[:, 0:3 * CHUNKS].bitcast(I32)
    srcf, dstf, relf, win, tile, din, junk, pick = part[3:11]
    bh = flat[:, 11 * CHUNKS:11 * CHUNKS + 3 * FEAT]
    before = flat[:, 11 * CHUNKS + 3 * FEAT:12 * CHUNKS + 3 * FEAT]
    beforef = flat[:, 12 * CHUNKS + 3 * FEAT:13 * CHUNKS + 3 * FEAT]
    pidx, thresh, count = k.st[0][:, 0:1], k.st[0][:, 1:2], k.st[0][:, 2:3]
    scratch = k.st[1]
    att = k.work[:, 0:2 * FEAT].rearrange("f (s n) -> f s n", s=2)
    prod = k.work[:, 2 * FEAT:4 * FEAT].rearrange("f (c n) -> f c n", c=KC)
    with nc.Block() as block:

        @block.sync
        def _(sp):
            for n, name in enumerate(("srcT", "dstT", "relT")):
                sp.dma_start(raw[:, CHUNKS * n:CHUNKS * (n + 1)], d[name][:, :]).then_inc(edges, 16)
            prev = before.bitcast(I32)
            sp.dma_start(prev[1:P, :], d["dstT"][0:P - 1, :]).then_inc(edges, 16)
            sp.dma_start(prev[0:1, 1:CHUNKS], d["dstT"][P - 1:P, 0:CHUNKS - 1]).then_inc(edges, 16)
            sp.dma_start(prev[0:1, 0:1], d["dstT"][0:1, 0:1]).then_inc(edges, 16)
            for c, name in enumerate(("attn_r", "attn_l")):
                sp.dma_start(att[:, c, :], d[name].partition_broadcast(128)).then_inc(loaded, 16)
            for sb, name in ((k.W1, "W1"), (k.W2, "W2"), (k.wih, "w_ihT"), (k.Wg, "WgT"),
                             (k.Wz[:, :, 0:FEAT], "weight")):
                sp.dma_start(sb[:, :, 0:FEAT * (3 if name[0:2] == "w_" else 1)],
                             d[name].rearrange("(c f) n -> f c n", f=128)).then_inc(loaded, 16)
            for sb, name in ((k.b1, "b1"), (k.b2, "b2"), (k.bg, "bg"), (k.gamma, "gamma"), (k.beta, "beta"),
                             (k.bi, "b_ih"), (bh, "b_hh"), (k.slope, "a")):
                sp.dma_start(sb[:, :], d[name].partition_broadcast(P)).then_inc(loaded, 16)
            sp.dma_start(k.rel[:, :], d["relv"][:, :]).then_inc(loaded, 16)

        @block.gpsimd
        def _(pool):
            g = nc.gpsimd
            g.memset(k.mhalf[:, :], -0.5)
            g.memset(k.ones[:, :], 1.0)
            g.iota(k.iota_keys, pattern=[[1, KW]], base=0, channel_multiplier=0, allow_small_or_imprecise_dtypes=True)
            g.iota(k.iota_lo, pattern=[[1, 128]], base=0, channel_multiplier=0, allow_small_or_imprecise_dtypes=True)
            g.iota(k.win_off, pattern=[[-P, 128]], base=0, channel_multiplier=0, allow_small_or_imprecise_dtypes=True)
            g.iota(pidx, pattern=[[0, 1]], base=0, channel_multiplier=1, allow_small_or_imprecise_dtypes=True)
            g.iota(thresh, pattern=[[0, 1]], base=0, channel_multiplier=WIN,
                   allow_small_or_imprecise_dtypes=True).then_inc(made, 1)

        @block.vector
        def _(dve):
            v = nc.vector
            stt = v.scalar_tensor_tensor
            own = Chain(dve, ok, 100).tile(0)
            v.memset(k.odeg8[:, :], 0.0)
            v.memset(k.blk[0][:, :].bitcast(U32), 0)
            v.memset(k.blk[1][:, :].bitcast(U32), 0)
            v.memset(k.row[0][:, :].bitcast(U32), 0)
            dve.wait_ge(made, 1)
            own.link(v.tensor_scalar(k.ident[:, :], k.iota_lo, pidx, None, ALU.is_equal))
            v.tensor_copy(k.identb[:, :], k.ident[:, :])
            own.link(v.tensor_scalar(scratch[:, 0:1], pidx, float(P - 1), None, ALU.is_equal))
            own.link(v.tensor_scalar(pick[:, 0:WINDOWS], k.ones[0:P, :], scratch[:, 0:1], None, ALU.mult))
            dve.wait_ge(edges, 96)
            v.tensor_copy(beforef, before.bitcast(I32))
            v.tensor_copy(srcf, raw[:, 0:CHUNKS])
            v.tensor_copy(dstf, raw[:, CHUNKS:2 * CHUNKS])
            own.link(v.tensor_copy(relf, raw[:, 2 * CHUNKS:3 * CHUNKS]))
            own.link(v.tensor_tensor(beforef, beforef, dstf, ALU.is_gt))
            own.link(v.tensor_reduce(scratch[:, 4:5], beforef, AX.X, ALU.add))
            dve.sem_inc(have_pick, 1)

            def floor_div(out, x, by):
                own.link(v.tensor_scalar(out, x, 0.5, 1.0 / by, ALU.add, ALU.mult))
                own.link(v.tensor_scalar(out, out, -0.5, None, ALU.add))
                own.link(v.tensor_scalar(out, out, 12582912.0, None, ALU.add))
                own.link(v.tensor_scalar(out, out, -12582912.0, None, ALU.add))

            floor_div(win, dstf, WIN)
            floor_div(tile, srcf, P)
            own.link(stt(out=k.lo_key, in0=win, scalar=float(P), in1=srcf, op0=ALU.mult, op1=ALU.add))
            own.link(stt(out=k.lo_key, in0=tile, scalar=-float(P), in1=k.lo_key, op0=ALU.mult, op1=ALU.add))
            own.link(stt(out=k.rel_key, in0=win, scalar=float(P), in1=relf, op0=ALU.mult, op1=ALU.add))
            own.link(stt(out=din, in0=win, scalar=-float(WIN), in1=dstf, op0=ALU.mult, op1=ALU.add))
            own.link(stt(out=k.hi_key, in0=tile, scalar=float(WIN), in1=din, op0=ALU.mult, op1=ALU.add))
            own.link(v.tensor_tensor(k.oh_din.rearrange("p (c n) -> p c n", n=WIN),
                                     k.iota_lo[:, 0:WIN].unsqueeze(1).to_broadcast([P, CHUNKS, WIN]),
                                     din.unsqueeze(2).to_broadcast([P, CHUNKS, WIN]), ALU.is_equal))
            dve.wait_ge(picked, 1)
            own.link(v.tensor_scalar(junk, k.ps[0:P, 0, 0:CHUNKS], thresh, 0.0, ALU.is_lt, ALU.add, accum_out=count))
            own.link(v.tensor_scalar(count, count, float(CHUNKS - 1), None, ALU.min))
            dve.sem_inc(have_count, 1)
            dve.wait_ge(loaded, 16 * 16)
            for side in range(2):
                for c in range(KC):
                    own.link(v.tensor_tensor(prod[:, c, :], k.Wz[:, c, 0:FEAT], att[:, side, :], ALU.mult))
                    own.link(v.tensor_reduce(k.Wz[:, c, FEAT + HEADS * side:FEAT + HEADS * (side + 1)],
                                             prod[:, c, :].rearrange("p (h n) -> p h n", n=DH), AX.X, ALU.add))
            own.link(stt(out=prod, in0=k.W1[:, :, :], scalar=-1.0, in1=k.W1[:, :, :], op0=ALU.mult, op1=ALU.max))
            dve.sem_inc(have_abs, 1)
            absb = junk[:, 0:FEAT]
            own.link(stt(out=absb, in0=k.b1[:, :], scalar=-1.0, in1=k.b1[:, :], op0=ALU.mult, op1=ALU.max))
            own.link(stt(out=scratch[:, 1:2], in0=k.slope[:, :], scalar=-1.0, in1=k.slope[:, :], op0=ALU.mult, op1=ALU.max))
            own.link(v.tensor_scalar(scratch[:, 1:2], scratch[:, 1:2], 1.0, None, ALU.max))
            dve.wait_ge(bound, 1)
            own.link(stt(out=absb, in0=k.ps[0:P, 2, 0:FEAT], scalar=16.0, in1=absb, op0=ALU.mult, op1=ALU.add))
            own.link(v.tensor_reduce(scratch[:, 0:1], absb, AX.X, ALU.max))
            own.link(v.tensor_scalar(scratch[:, 0:1], scratch[:, 0:1], scratch[:, 1:2], None, ALU.mult))
            own.link(v.tensor_scalar(scratch[:, 0:1], scratch[:, 0:1], 2.0 ** -60, None, ALU.max))
            own.link(v.tensor_scalar(scratch[:, 2:3].bitcast(I32), scratch[:, 0:1].bitcast(I32), 0x7F800000, None,
                                     ALU.bitwise_and))
            own.link(v.tensor_scalar(scratch[:, 3:4], scratch[:, 2:3], 2.0 ** -14, None, ALU.mult))
            own.link(v.reciprocal(k.gscale[:, :], scratch[:, 3:4]))
            own.link(v.tensor_scalar(k.gunscale[:, :], scratch[:, 3:4], CNT, None, ALU.mult))
            own.link(v.tensor_tensor(k.gslope[:, :], k.gscale[:, :], k.slope[:, :], ALU.mult))
            own.link(v.tensor_tensor(k.bi[:, 0:2 * FEAT], k.bi[:, 0:2 * FEAT], bh[:, 0:2 * FEAT], ALU.add))
            own.link(v.tensor_copy(k.bhn[:, :], bh[:, 2 * FEAT:3 * FEAT]))
            dve.wait_ge(turned, 1)
            some, none = scratch[0:1, 5:6], scratch[0:1, 6:7]
            first, last = junk[0:1, 0:WINDOWS], junk[0:1, 128:128 + WINDOWS]
            own.link(v.tensor_scalar(some, k.ps[0:1, 3, 0:1], 0.0, None, ALU.is_gt))
            own.link(v.tensor_scalar(none, some, -1.0, 1.0, ALU.mult, ALU.add))
            own.link(v.tensor_copy(first, k.ps[0:1, 1, 0:WINDOWS]))
            own.link(v.tensor_scalar(k.table[0:1, 0:WINDOWS], first, none, None, ALU.mult))
            own.link(v.memset(last[:, WINDOWS - 1:WINDOWS], CHUNKS - 1))
            own.link(v.tensor_copy(last[:, 0:WINDOWS - 1], first[:, 1:WINDOWS]))
            own.link(v.tensor_scalar(first, last, -1.0, float(CHUNKS - 1), ALU.mult, ALU.add))
            own.link(stt(out=k.table[0:1, 128:128 + WINDOWS], in0=first, scalar=some, in1=last, op0=ALU.mult, op1=ALU.add))
            own.link(v.tensor_scalar(some, some, float(CHUNKS - 1), 1.0, ALU.mult, ALU.add))
            own.link(v.tensor_scalar(k.table[0:1, 256:256 + WINDOWS], k.iota_lo[0:1, 0:WINDOWS], some, None, ALU.mult))

        @block.tensor
        def _(pe):
            pe.wait_ge(have_pick, 1)
            pe.matmul(k.ps[0:P, 0, 0:CHUNKS], pick[:, 0:P], dstf, start=True, stop=True)
            pe.matmul(k.ps[0:1, 3, 0:1], scratch[:, 4:5], k.ones[0:P, 0:1], start=True, stop=True).then_inc(picked, 1)
            pe.wait_ge(have_count, 1)
            pe.matmul(k.ps[0:1, 1, 0:P], count, k.ident[:, 0:P], start=True, stop=True).then_inc(turned, 1)
            pe.wait_ge(have_abs, 1)
            for c in range(KC):
                last = pe.matmul(k.ps[0:P, 2, 0:FEAT], k.ones[:, :], prod[:, c, :], start=(c == 0), stop=(c == KC - 1))
            last.then_inc(bound, 1)


def build(k):
    nc, d = k.nc, k.d
    x_loaded, h_stored = k.sems("build_x"), k.sems("build_h")
    hot, freed = k.sem("build_hot"), k.sem("build_freed")
    evicted, ct_evicted, put, ored = (k.sem("build_" + n) for n in ("evicted", "ct_evicted", "put", "ored"))
    var_ready, rstd_ready, nmr_ready = k.sem("build_var"), k.sem("build_rstd"), k.sem("build_nmr")
    h_ready, hi_ready, lo_ready = k.sem("build_h"), k.sem("build_hi"), k.sem("build_lo")
    c_dve, c_act = k.sem("build_c_dve"), k.sem("build_c_act")

    def chunks_of(eng, n):
        return (eng.value_load(k.table[0:1, bass.ds(n, 1)], min_val=0, max_val=CHUNKS - 1),
                eng.value_load(k.table[0:1, bass.ds(n + 128, 1)], min_val=0, max_val=CHUNKS - 1),
                eng.value_load(k.table[0:1, bass.ds(n + 256, 1)], min_val=0, max_val=CHUNKS * WINDOWS))

    with nc.Block() as block:

        @block.sync
        def _(sp):
            def load_x(i, par, half):
                wait_past(sp, h_ready, i - 1)
                settle(sp, k)
                sp.dma_start(k.xin[par][:, :], rows(d["x"], i)).then_inc(x_loaded[par], 16)

            def store_h(i, par, half):
                sp.wait_ge(h_ready, i + 1)
                settle(sp, k)
                sp.dma_start(rows(d["h0"], i), k.ho[par][:, :]).then_inc(h_stored[par], 16)

            pipelined(sp, [(0, load_x), (1, store_h)])
            for par in range(2):
                sp.wait_ge(h_stored[par], 16 * ((TILES + 1 - par) // 2))

        @block.gpsimd
        def _(pool):
            g = nc.gpsimd

            def put_block(b, par, half):
                pool.wait_ge(evicted, WPT * (b + 1) + 2)
                g.tensor_copy(k.adj[:, :, :].bitcast(U32)[:, :, bass.ds(b * WORDS, WORDS)],
                              k.blk[par][:, :].bitcast(U32).rearrange("p (j w) -> p j w", w=WORDS)).then_inc(put, 1)

            def root(i, par, half):
                pool.wait_ge(var_ready, i + 1)
                g.tensor_tensor(k.st[par][:, 9:10], k.st[par][:, 8:9], k.mhalf[:, 0:1], ALU.pow).then_inc(rstd_ready, 1)

            pipelined(pool, [(1, put_block), (0, root)])

        @block.vector
        def _(dve):
            v = nc.vector
            own = Chain(dve, c_dve, 2)

            def one_hots(b, par, half):
                for q in range(WPT):
                    n = WPT * b + q
                    lo, hi, offset = chunks_of(dve, n)
                    with dve.Fori(lo, hi + 1) as c:
                        t = c + offset
                        slot = t % SLOTS
                        dve.wait_ge(freed, t + 1)
                        v.tensor_scalar(k.oh_keys[:, bass.ds(slot * KW, KEYS + 1)], k.iota_keys[:, 0:KEYS + 1],
                                        k.hi_key[:, bass.ds(c, 1)], None, ALU.is_equal)
                        v.tensor_scalar(k.oh_rel[:, bass.ds(slot * 16, RELS)], k.iota_lo[:, 0:RELS],
                                        k.rel_key[:, bass.ds(c, 1)], k.win_off[:, bass.ds(n, 1)],
                                        ALU.subtract, ALU.is_equal)
                        v.tensor_scalar(k.oh_lo[:, bass.ds(slot * 128, P)], k.iota_lo[:, 0:P],
                                        k.lo_key[:, bass.ds(c, 1)], k.win_off[:, bass.ds(n, 1)],
                                        ALU.subtract, ALU.is_equal).then_inc(hot, 1)

            def or_block(b, par, half):
                dve.wait_ge(evicted, WPT * (b + 1) + 2)
                if not isinstance(b, int) or b > 0:
                    dve.wait_ge(ored, b)
                v.tensor_tensor(k.over, k.over, k.blk[par][:, :].bitcast(U32), ALU.bitwise_or).then_inc(ored, 1)

            def stats(i, par, half):
                own.tile(i)
                dve.wait_ge(x_loaded[par], 16 * (half + 1))
                wait_past(dve, nmr_ready, i - 1)
                own.link(v.bn_stats(k.st[par][:, 0:6], k.xin[par][:, :]))
                settle(dve, k)
                own.link(v.bn_aggr(k.st[par][:, 6:8], k.st[par][:, 0:6]))
                v.tensor_scalar(k.st[par][:, 8:9], k.st[par][:, 7:8], EPS, None, ALU.add).then_inc(var_ready, 1)

            def shift(i, par, half):
                dve.wait_ge(rstd_ready, i + 1)
                v.tensor_scalar(k.st[par][:, 10:11], k.st[par][:, 6:7], k.st[par][:, 9:10], -1.0,
                                ALU.mult, ALU.mult).then_inc(nmr_ready, 1)

            def low(i, par, half):
                dve.wait_ge(hi_ready, i + 1)
                v.scalar_tensor_tensor(out=k.pairA[:, bass.ds(i, 1), FEAT:2 * FEAT], in0=k.ho[par][:, :].unsqueeze(1), scalar=UP,
                                       in1=k.pairA[:, bass.ds(i, 1), 0:FEAT], op0=ALU.mult,
                                       op1=ALU.subtract).then_inc(lo_ready, 1)

            pipelined(dve, [(0, one_hots), (1, or_block), (0, stats), (1, shift), (3, low)])

        @block.scalar
        def _(act):
            s = nc.scalar
            act.sem_inc(evicted, 2)
            act.sem_inc(ct_evicted, 2)
            own = Chain(act, c_act, 1)

            def evict(b, par, half):
                wait_past(act, put, b - 1)
                wait_past(act, ored, b - 1)
                for q in range(WPT):
                    n = WPT * b + q
                    _, last_chunk, offset = chunks_of(act, n)
                    act.wait_ge(freed, last_chunk + offset + 1 + SLOTS)
                    settle(act, k)
                    bank = 2 * ((par + q) % 2)
                    out = k.blk[par][:, :].rearrange("p (j c) -> p j c", c=PITCH)[:, :, WIN * q:WIN * (q + 1)]
                    for a, (j0, j1) in enumerate(((0, HALF_A), (HALF_A, TILES))):
                        last = s.activation(out[:, j0:j1, :], k.ps[0:P, bank + a, 0:(j1 - j0) * WIN]
                                            .rearrange("p (j n) -> p j n", n=WIN), ACT.Copy, scale=1.0 / CNT,
                                            saturate=False)
                    last.then_inc(evicted, 1)
                s.copy(k.CT[:, bass.ds(b, 1), :], k.ps[0:RELS, 4 + par, 0:P].unsqueeze(1)).then_inc(ct_evicted, 1)

            def h(i, par, half):
                act.wait_ge(nmr_ready, i + 1)
                if not isinstance(half, int) or half > 0:
                    act.wait_ge(h_stored[par], 16 * half)
                wait_past(act, lo_ready, i - 1)
                s.activation(k.ho[par][:, :], k.xin[par][:, :], ACT.Relu, bias=k.st[par][:, 10:11],
                             scale=k.st[par][:, 9:10]).then_inc(h_ready, 1)
                act.wait_ge(h_ready, i + 1)
                s.activation(k.pairA[:, bass.ds(i, 1), 0:FEAT], k.ho[par][:, :].unsqueeze(1), ACT.Copy, scale=UP).then_inc(hi_ready, 1)

            pipelined(act, [(0, evict), (1, h)])

        @block.tensor
        def _(pe):
            pe.sem_inc(freed, SLOTS)

            def step(c, offset, bank, par, q, start):
                t = c + offset
                slot = t % SLOTS
                pe.wait_ge(hot, t + 1)
                lhs = k.oh_lo[:, bass.ds(slot * 128, P)]
                for a, (j0, j1) in enumerate(((0, HALF_A), (HALF_A, TILES))):
                    pe.matmul(k.ps[0:P, bank + a, 0:(j1 - j0) * WIN], lhs,
                              k.oh_keys[:, bass.ds(slot * KW + j0 * WIN, (j1 - j0) * WIN)],
                              start=start, stop=True, skip_group_check=True)
                pe.matmul(k.ps[0:RELS, 4 + par, WIN * q:WIN * (q + 1)], k.oh_rel[:, bass.ds(slot * 16, RELS)],
                          k.oh_din[:, bass.ds(c * WIN, WIN)], start=start, stop=True,
                          skip_group_check=True).then_inc(freed, 1)

            def windows(b, par, half):
                pe.wait_ge(ct_evicted, b + 1)
                for q in range(WPT):
                    n = WPT * b + q
                    lo, hi, offset = chunks_of(pe, n)
                    pe.wait_ge(evicted, n + 1)
                    bank = 2 * ((par + q) % 2)
                    step(lo, offset, bank, par, q, True)
                    with pe.If(hi > lo):
                        with pe.Fori(lo + 1, hi + 1) as c:
                            step(c, offset, bank, par, q, False)
                    with pe.Else():
                        pass

            pipelined(pe, [(0, windows)])


def degrees(k):
    nc = k.nc
    summed, have_b, have_viol, voted, root = (k.sem("deg_" + n) for n in ("summed", "have_b", "have_viol", "voted", "root"))
    ok, cleared = k.sem("deg_ok"), k.sem("deg_cleared")
    with nc.Block() as block:

        @block.tensor
        def _(pe):
            for i in range(TILES):
                last = pe.matmul(k.ps[0:P, 0, i:i + 1], k.CT[:, i, :], k.ones[0:RELS, 0:1], start=True, stop=True)
            last.then_inc(summed, 1)
            pe.wait_ge(have_viol, 1)
            pe.matmul(k.ps[0:1, 1, 0:2], k.ones[0:P, 0:1], k.st[0][:, 0:2], start=True, stop=True).then_inc(voted, 1)

        @block.gpsimd
        def _(pool):
            pool.wait_ge(have_b, 1)
            nc.gpsimd.tensor_tensor(k.dinv[:, 0:TILES], k.dinv[:, 0:TILES], k.mhalf[:, 0:TILES], ALU.pow).then_inc(root, 1)

        @block.vector
        def _(dve):
            v = nc.vector
            own = Chain(dve, ok, 100).tile(0)
            n = slice(0, TILES)
            dve.wait_ge(summed, 1)
            own.link(v.tensor_copy(k.indeg[:, n], k.ps[0:P, 0, n]))
            own.link(v.tensor_scalar(k.dinv[:, n], k.indeg[:, n], 1.0, None, ALU.add))
            dve.sem_inc(have_b, 1)
            own.link(v.tensor_reduce(k.st[0][:, 1:2], k.indeg[:, n], AX.X, ALU.add))
            own.link(v.tensor_scalar(k.over, k.over, 0x40404040, None, ALU.bitwise_and))
            own.link(v.tensor_reduce(k.st[0][:, 0:1], k.over, AX.X, ALU.max))
            dve.sem_inc(have_viol, 1)
            own.link(v.tensor_scalar(k.rsB[:, n], k.indeg[:, n], 1.0, None, ALU.max))
            own.link(v.reciprocal(k.rsB[:, n], k.rsB[:, n]))
            own.link(v.tensor_scalar(k.rsD[:, n], k.indeg[:, n], 0.0, CNT, ALU.is_gt, ALU.mult))
            own.link(v.tensor_tensor(k.rsB[:, n], k.rsB[:, n], k.rsD[:, n], ALU.mult))
            dve.wait_ge(root, 1)
            own.link(v.tensor_scalar(k.dinvs[:, n], k.dinv[:, n], CNT / UP, None, ALU.mult))
            own.link(v.tensor_scalar(k.dinvu[:, n], k.dinv[:, n], UP, None, ALU.mult))
            dve.wait_ge(voted, 1)
            own.link(v.tensor_scalar(k.st[1][0:1, 0:1], k.ps[0:1, 1, 1:2], float(EDGES), None, ALU.not_equal))
            own.link(v.tensor_scalar(k.st[1][0:1, 1:2], k.ps[0:1, 1, 0:1], 0.0, None, ALU.is_gt))
            own.link(v.tensor_tensor(k.flag[:, :], k.st[1][0:1, 0:1], k.st[1][0:1, 1:2], ALU.max))

            def run(general):
                if general:
                    v.memset(k.adj[:, :, :].bitcast(U32), 0).then_inc(cleared, 1)
                    dve.wait_ge(cleared, 1)

            either(dve, k, run)


def split_scaled(k, s, dst, i, t, scale):
    return s.activation(dst[:, bass.ds(i, 1), 0:FEAT], t[:, :].unsqueeze(1), ACT.Copy, scale=scale)


def mean_by_destination(k, name, src, dst, store, second):
    nc = k.nc
    acc_ready, acc_free, copied = (k.sem(f"{name}_{n}") for n in ("acc", "acc_free", "copied"))
    aw_ready, t_ready, hi_ready, lo_ready = (k.sem(f"{name}_{n}") for n in ("aw", "t", "hi", "lo"))
    stored = k.sems(name + "_stored")
    whh_loaded = k.sem(name + "_whh") if second else None
    extra_ready = k.sems(name + "_extra")
    with nc.Block() as block:

        @block.sync
        def _(sp):
            def put(i, par, half):
                sp.wait_ge(t_ready, i + 1)
                settle(sp, k)
                sp.dma_start(rows(store, i), k.t[par][:, :]).then_inc(stored[par], 16)

            if second:
                sp.dma_start(k.whh[:, :, :], k.d["w_hhT"].rearrange("(c f) n -> f c n", f=128)).then_inc(whh_loaded, 16)
            either(sp, k, lambda general: pipelined(sp, (
                [(0, extra_loads(k, sp, acc_ready, extra_ready))] if general else []) + [(0, put)]))
            finish_stores(sp, stored)
            if second:
                sp.wait_ge(whh_loaded, 16)

        @block.gpsimd
        def _(pool):
            stage_columns(k, pool, copied, acc_ready)

        @block.tensor
        def _(pe):
            def run(general):
                def agg(i, par, half):
                    pe.wait_ge(copied, i + 1)
                    wait_past(pe, t_ready, i - 1)
                    aggregate(k, pe, par, half, src, extra_ready if general else None).then_inc(acc_ready, 1)

                pipelined(pe, [(0, agg)])

            either(pe, k, run)

        @block.scalar
        def _(act):
            def scale_high(i, par, half):
                act.wait_ge(acc_ready, i + 1)
                wait_past(act, t_ready, i - 1)
                nc.scalar.activation(k.aw[par][:, :], k.ps[0:P, par, 0:FEAT], ACT.Copy,
                                     scale=k.rsB[:, bass.ds(i, 1)]).then_inc(aw_ready, 1)
                act.wait_ge(t_ready, i + 1)
                split_scaled(k, nc.scalar, dst, i, k.t[par], 1.0).then_inc(hi_ready, 1)

            pipelined(act, [(0, scale_high)])

        @block.vector
        def _(dve):
            v = nc.vector

            def combine(i, par, half):
                dve.wait_ge(aw_ready, i + 1)
                if not isinstance(half, int) or half > 0:
                    dve.wait_ge(stored[par], 16 * half)
                v.scalar_tensor_tensor(out=k.t[par][:, :], in0=k.ps[0:P, par, FEAT:2 * FEAT],
                                       scalar=k.rsB[:, bass.ds(i, 1)], in1=k.aw[par][:, :],
                                       op0=ALU.mult, op1=ALU.add).then_inc(t_ready, 1)
                dve.wait_ge(hi_ready, i + 1)
                v.tensor_tensor(dst[:, bass.ds(i, 1), FEAT:2 * FEAT], k.t[par][:, :].unsqueeze(1),
                                dst[:, bass.ds(i, 1), 0:FEAT], ALU.subtract).then_inc(lo_ready, 1)

            pipelined(dve, [(0, combine)])


def stage_columns(k, pool, copied, used):
    def copy(i, par, half):
        wait_past(pool, used, i - 1)
        k.nc.gpsimd.tensor_copy(k.blk[par][:, :].bitcast(U32).rearrange("p (j w) -> p j w", w=WORDS),
                                k.adj[:, :, :].bitcast(U32)[:, :, bass.ds(i * WORDS, WORDS)]).then_inc(copied, 1)

    pipelined(pool, [(0, copy)])


def aggregate(k, pe, par, half, src, extra_ready=None):
    settle(pe, k)
    a = k.blk[par][:, :].rearrange("p (j c) -> p j c", c=PITCH)
    for j in range(TILES):
        if j == TILES - 1 and extra_ready is not None:
            pe.wait_ge(extra_ready[par], 16 * (half + 1))
            pe.matmul(k.ps[0:P, par, 0:FEAT], k.ident[:, 0:P], k.extra[par][:, :], start=False, stop=False)
        last = pe.matmul(k.ps[0:P, par, :], a[:, j, 0:P], src[:, j, :], start=(j == 0), stop=(j == TILES - 1))
    return last


def extra_loads(k, sp, acc, extra_ready):
    def load_extra(i, par, half):
        wait_past(sp, acc, i - 1)
        settle(sp, k)
        sp.dma_start(k.extra[par][:, :], rows(k.d["extra"], i)).then_inc(extra_ready[par], 16)

    return load_extra


def finish_stores(eng, stored):
    for par in range(2):
        eng.wait_ge(stored[par], 16 * ((TILES + 1 - par) // 2))


def wait_slot(eng, sems, par, half):
    if not isinstance(half, int) or half > 0:
        eng.wait_ge(sems[par], 16 * half)


def turn(k, pe, s, i, par, bank, at, tile, turned_to):
    for c in range(KC):
        last = pe.transpose(k.ps[0:128, bank, at + c * P:at + (c + 1) * P], tile[:, 128 * c:128 * (c + 1)], k.ident[:, 0:P])
    return last


def product(k, pe, out, tT, w):
    for c in range(KC):
        last = pe.matmul(out, tT[:, c, :], w[:, c, :], start=(c == 0), stop=(c == KC - 1))
    return last


def scatter_mean(k, name, src, first):
    nc, d = k.nc, k.d
    S = {n: k.sem(f"{name}_{n}") for n in (
        "row", "flipped", "flip_a", "flip_v", "degree", "scale", "blk", "acc", "aw", "t", "turned", "tT", "product",
        "u", "p", "x", "hi", "lo", "var", "rstd", "nmr", "h", "own_a", "own_v", "own_w")}
    kept, loaded_b = k.sems(name + "_kept"), k.sems(name + "_loaded_b")
    loaded_x, stored_x, stored_h = k.sems(name + "_loaded_x"), k.sems(name + "_stored_x"), k.sems(name + "_stored_h")
    W, bias = (k.W1, k.b1) if first else (k.W2, k.b2)
    agg_lag = 1 if first else 0
    rs = k.rsD if first else k.rsD4
    extra_ready = k.sems(name + "_extra")
    GROUPS = [(4 * g, min(4 * g + 4, TILES)) for g in range((TILES + 3) // 4)]

    with nc.Block() as block:

        @block.sync
        def _(sp):
            def keep_block(i, par, half):
                sp.wait_ge(S["flip_a"], 4 * (i + 1))
                settle(sp, k)
                sp.wait_ge(S["flip_v"], 3 * (i + 1))
                settle(sp, k)
                sp.dma_start(d["adjT"][bass.ds(i, 1), :, :].rearrange("o p w -> p (o w)"),
                             k.blk[par][:, :].bitcast(U32)).then_inc(kept[par], 16)

            def load_block(i, par, half):
                wait_past(sp, S["acc"], i - 1)
                settle(sp, k)
                sp.dma_start(k.blk[par][:, :].bitcast(U32),
                             d["adjT"][bass.ds(i, 1), :, :].rearrange("o p w -> p (o w)")).then_inc(loaded_b[par], 16)

            def load_xh(i, par, half):
                wait_past(sp, S["x"], i - 1)
                settle(sp, k)
                sp.dma_start(k.xin[par][:, :], rows(d["x"], i)).then_inc(loaded_x[par], 16)
                sp.dma_start(k.hin[par][:, :], rows(d["h0"], i)).then_inc(loaded_x[par], 16)

            def store_g(i, par, half):
                sp.wait_ge(S["x"], i + 1)
                settle(sp, k)
                sp.dma_start(rows(d["g"], i), k.xo[par][:, :]).then_inc(stored_x[par], 16)

            def store_x(i, par, half):
                sp.wait_ge(S["x"], i + 1)
                settle(sp, k)
                sp.dma_start(rows(d["x1"], i), k.xo[par][:, :]).then_inc(stored_x[par], 16)
                sp.wait_ge(S["h"], i + 1)
                settle(sp, k)
                sp.dma_start(rows(d["h1"], i), k.ho[par][:, :]).then_inc(stored_h[par], 16)

            stages = [(0, keep_block), (3, store_g)] if first else [(0, load_block), (0, load_xh), (2, store_x)]
            either(sp, k, lambda general: pipelined(sp, (
                [(agg_lag, extra_loads(k, sp, S["acc"], extra_ready))] if general else []) + stages))
            finish_stores(sp, kept if first else stored_h)
            finish_stores(sp, stored_x)

        @block.gpsimd
        def _(pool):
            def copy_row(i, par, half):
                wait_past(pool, S["flipped"], len(GROUPS) * (i - 1))
                wait_past(pool, S["degree"], i - 1)
                nc.gpsimd.tensor_copy(k.row[par][:, :].bitcast(U32),
                                      k.adj[:, bass.ds(i, 1), :].bitcast(U32).rearrange("p o w -> p (o w)")
                                      ).then_inc(S["row"], 1)

            def root(i, par, half):
                pool.wait_ge(S["var"], i + 1)
                nc.gpsimd.tensor_tensor(k.st[par][:, 9:10], k.st[par][:, 8:9], k.mhalf[:, 0:1],
                                        ALU.pow).then_inc(S["rstd"], 1)

            pipelined(pool, [(0, copy_row)] if first else [(0, root)])

        @block.tensor
        def _(pe):
            def run(general):
                def flip(i, par, half):
                    pe.wait_ge(S["row"], i + 1)
                    row = k.row[par][:, :].rearrange("p (j c) -> p j c", c=PITCH)
                    for g, (j0, j1) in enumerate(GROUPS):
                        sem, n = (("flip_a", 4 * i + (-1, 0, 1, 2)[g // 2]) if g % 2 == 0 else
                                  ("flip_v", 3 * i + (0, -1, 1)[g // 2]))
                        wait_past(pe, S[sem], n)
                        settle(pe, k)
                        for j in range(j0, j1):
                            last = pe.matmul(k.ps[0:P, 4 + g % 4, (j - j0) * P:(j - j0 + 1) * P], row[:, j, 0:P],
                                             k.identb[:, 0:P], start=True, stop=True)
                        last.then_inc(S["flipped"], 1)

                def agg(i, par, half):
                    if first:
                        pe.wait_ge(S["flip_a"], 4 * (i + 1))
                        pe.wait_ge(S["flip_v"], 3 * (i + 1))
                    else:
                        pe.wait_ge(loaded_b[par], 16 * (half + 1))
                    wait_past(pe, S["t"], i - 1)
                    aggregate(k, pe, par, half, src, extra_ready if general else None).then_inc(S["acc"], 1)

                def turn_t(i, par, half):
                    pe.wait_ge(S["t"], i + 1)
                    wait_past(pe, S["tT"], i)
                    turn(k, pe, S, i, par, 2, 0, k.t[par], None).then_inc(S["turned"], 1)

                def dense(i, par, half):
                    pe.wait_ge(S["tT"], i + 1)
                    wait_past(pe, S["u"], i)
                    product(k, pe, k.ps[0:P, 3, 0:FEAT], k.tT[par], W).then_inc(S["product"], 1)

                pipelined(pe, ([(0, flip)] if first else []) + [(agg_lag, agg), (agg_lag + 1, turn_t), (agg_lag + 2, dense)])

            either(pe, k, run)

        @block.scalar
        def _(act):
            s = nc.scalar

            def flip_out(i, par, half):
                wait_past(act, S["acc"], i - 1)
                wait_slot(act, kept, par, half)
                blk = k.blk[par][:, :].rearrange("p (j c) -> p j c", c=PITCH)
                for g in (0, 2, 4, 6):
                    j0, j1 = GROUPS[g]
                    act.wait_ge(S["flipped"], len(GROUPS) * i + g + 1)
                    settle(act, k)
                    s.activation(blk[:, j0:j1, 0:P], k.ps[0:P, 4 + g % 4, 0:(j1 - j0) * P].rearrange("p (j c) -> p j c", c=P),
                                 ACT.Copy, saturate=False).then_inc(S["flip_a"], 1)

            own_a = Chain(act, S["own_a"], 1)

            def degree(i, par, half):
                act.wait_ge(S["row"], i + 1)
                wait_past(act, S["scale"], i - 1)
                settle(act, k)
                s.activation(k.junk[:, :], k.row[par][:, :], ACT.Copy, saturate=False,
                             accum_out=k.st[par][:, 14:15]).then_inc(S["degree"], 1)

            def scale_high(i, par, half):
                act.wait_ge(S["acc"], i + 1)
                if first:
                    act.wait_ge(S["scale"], i + 1)
                wait_past(act, S["t"], i - 1)
                s.activation(k.aw[par][:, :], k.ps[0:P, par, 0:FEAT], ACT.Copy,
                             scale=rs[:, bass.ds(i, 1)]).then_inc(S["aw"], 1)

            def tT_out(i, par, half):
                act.wait_ge(S["turned"], i + 1)
                wait_past(act, S["product"], i - 1)
                s.copy(k.tT[par][:, 0:KC, :], k.ps[0:128, 2, 0:2 * P]
                       .rearrange("f (c p) -> f c p", p=P)).then_inc(S["tT"], 1)

            def positive(i, par, half):
                act.wait_ge(S["u"], i + 1)
                if first:
                    s.activation(k.ho[par][:, :], k.hin[par][:, :], ACT.Relu, scale=k.gscale[:, :]).then_inc(S["p"], 1)
                    act.wait_ge(S["x"], i + 1)
                    split_scaled(k, s, k.pairA, i, k.xo[par], 1.0).then_inc(S["hi"], 1)
                else:
                    wait_slot(act, stored_h, par, half)
                    s.activation(k.ho[par][:, :], k.hin[par][:, :], ACT.Relu).then_inc(S["p"], 1)
                    act.wait_ge(S["nmr"], i + 1)
                    s.activation(k.ho[par][:, :], k.xo[par][:, :], ACT.Relu, bias=k.st[par][:, 10:11],
                                 scale=k.st[par][:, 9:10]).then_inc(S["h"], 1)
                    act.wait_ge(S["h"], i + 1)
                    split_scaled(k, s, k.pairA, i, k.ho[par], UP).then_inc(S["hi"], 1)

            pipelined(act, ([(0, flip_out), (0, degree)] if first else []) +
                      [(agg_lag, scale_high), (agg_lag + 1, tT_out), (agg_lag + 2, positive)])

        @block.vector
        def _(dve):
            v = nc.vector
            stt = v.scalar_tensor_tensor
            own_v = Chain(dve, S["own_v"], 4)
            own_w = Chain(dve, S["own_w"], 1 if first else 5)

            def flip_out(i, par, half):
                wait_past(dve, S["acc"], i - 1)
                wait_slot(dve, kept, par, half)
                blk = k.blk[par][:, :].rearrange("p (j c) -> p j c", c=PITCH)
                for g in (1, 3, 5):
                    j0, j1 = GROUPS[g]
                    dve.wait_ge(S["flipped"], len(GROUPS) * i + g + 1)
                    settle(dve, k)
                    v.tensor_copy(blk[:, j0:j1, 0:P], k.ps[0:P, 4 + g % 4, 0:(j1 - j0) * P]
                                  .rearrange("p (j c) -> p j c", c=P), saturate=False).then_inc(S["flip_v"], 1)

            def scale(i, par, half):
                own_v.tile(i)
                dve.wait_ge(S["degree"], i + 1)
                q, r = k.st[par][:, 15:16], k.st[par][:, 12:13]
                own_v.link(v.tensor_tensor(q, k.st[par][:, 14:15], k.odeg8[:, bass.ds(i, 1)], ALU.add))
                own_v.link(v.tensor_scalar(r, q, 1.0 / CNT, UP, ALU.max, ALU.mult))
                own_v.link(v.reciprocal(r, r))
                own_v.link(v.tensor_scalar(k.st[par][:, 13:14], q, 0.0, None, ALU.is_gt))
                v.tensor_tensor(k.rsD[:, bass.ds(i, 1)], r, k.st[par][:, 13:14], ALU.mult).then_inc(S["scale"], 1)

            def combine(i, par, half):
                dve.wait_ge(S["aw"], i + 1)
                wait_past(dve, S["turned"], i - 1)
                stt(out=k.t[par][:, :], in0=k.ps[0:P, par, FEAT:2 * FEAT], scalar=rs[:, bass.ds(i, 1)],
                    in1=k.aw[par][:, :], op0=ALU.mult, op1=ALU.add).then_inc(S["t"], 1)

            def after_g(i, par, half):
                own_w.tile(i)
                ps = k.ps[0:P, 3, 0:FEAT]
                u, p, g = k.hin[par], k.ho[par], k.xo[par]
                dve.wait_ge(S["product"], i + 1)
                v.tensor_tensor(u[:, :], ps, bias[:, :], ALU.add).then_inc(S["u"], 1)
                dve.wait_ge(S["p"], i + 1)
                own_w.link(v.tensor_scalar(u[:, :], u[:, :], 0.0, k.gslope[:, :], ALU.min, ALU.mult))
                wait_slot(dve, stored_x, par, half)
                wait_past(dve, S["hi"], i - 1)
                v.tensor_tensor(g[:, :], u[:, :], p[:, :], ALU.add).then_inc(S["x"], 1)
                dve.wait_ge(S["hi"], i + 1)
                v.tensor_tensor(k.pairA[:, bass.ds(i, 1), FEAT:2 * FEAT], g[:, :].unsqueeze(1),
                                k.pairA[:, bass.ds(i, 1), 0:FEAT], ALU.subtract).then_inc(S["lo"], 1)

            def after_x(i, par, half):
                own_w.tile(i)
                ps = k.ps[0:P, 3, 0:FEAT]
                u, p, x, st = k.hin[par], k.ho[par], k.xo[par], k.st[par]
                dve.wait_ge(loaded_x[par], 32 * (half + 1))
                own_w.link(v.tensor_tensor(u[:, :], u[:, :], bias[:, :], ALU.add))
                dve.wait_ge(S["product"], i + 1)
                v.tensor_tensor(u[:, :], ps, u[:, :], ALU.add).then_inc(S["u"], 1)
                dve.wait_ge(S["p"], i + 1)
                own_w.link(v.tensor_scalar(u[:, :], u[:, :], 0.0, k.slope[:, :], ALU.min, ALU.mult))
                wait_slot(dve, stored_x, par, half)
                own_w.link(v.tensor_tensor(x[:, :], u[:, :], p[:, :], ALU.add))
                v.tensor_tensor(x[:, :], x[:, :], k.xin[par][:, :], ALU.add).then_inc(S["x"], 1)
                dve.wait_ge(S["x"], i + 1)
                own_w.link(v.bn_stats(st[:, 0:6], x[:, :]))
                settle(dve, k)
                own_w.link(v.bn_aggr(st[:, 6:8], st[:, 0:6]))
                v.tensor_scalar(st[:, 8:9], st[:, 7:8], EPS, None, ALU.add).then_inc(S["var"], 1)
                dve.wait_ge(S["rstd"], i + 1)
                v.tensor_scalar(st[:, 10:11], st[:, 6:7], st[:, 9:10], -1.0, ALU.mult, ALU.mult).then_inc(S["nmr"], 1)
                dve.wait_ge(S["hi"], i + 1)
                stt(out=k.pairA[:, bass.ds(i, 1), FEAT:2 * FEAT], in0=k.ho[par][:, :].unsqueeze(1), scalar=UP,
                    in1=k.pairA[:, bass.ds(i, 1), 0:FEAT], op0=ALU.mult, op1=ALU.subtract).then_inc(S["lo"], 1)

            pipelined(dve, ([(0, flip_out), (0, scale)] if first else []) +
                      [(agg_lag, combine), (agg_lag + 2, after_g if first else after_x)])
            if first:
                dve.wait_ge(S["scale"], TILES)
                v.tensor_scalar(k.rsD4[:, 0:TILES], k.rsD[:, 0:TILES], UP / CNT, k.gunscale[:, :],
                                ALU.mult, ALU.mult).then_inc(S["scale"], 1)
                dve.wait_ge(S["scale"], TILES + 1)


def gru(k):
    nc, d = k.nc, k.d
    S = {n: k.sem("gru_" + n) for n in ("copied", "acc", "aw", "t", "turned", "tT", "product", "u", "p", "x", "hi",
                                        "lo", "var", "rstd", "nmr", "h", "rz", "gates", "pre", "new", "own")}
    extra_ready = k.sems("gru_extra")
    loaded, stored_x, stored_h = k.sems("gru_loaded"), k.sems("gru_stored_x"), k.sems("gru_stored_h")
    with nc.Block() as block:

        @block.sync
        def _(sp):
            def load(i, par, half):
                wait_past(sp, S["x"], i - 1)
                settle(sp, k)
                sp.dma_start(k.xin[par][:, :], rows(d["x1"], i)).then_inc(loaded[par], 16)
                sp.dma_start(k.hin[par][:, :], rows(d["h1"], i)).then_inc(loaded[par], 16)

            def store(i, par, half):
                sp.wait_ge(S["x"], i + 1)
                settle(sp, k)
                sp.dma_start(rows(d["x2"], i), k.xo[par][:, :]).then_inc(stored_x[par], 16)
                sp.wait_ge(S["h"], i + 1)
                settle(sp, k)
                sp.dma_start(rows(d["s2"], i), k.ho[par][:, :]).then_inc(stored_h[par], 16)

            either(sp, k, lambda general: pipelined(sp, (
                [(0, extra_loads(k, sp, S["acc"], extra_ready))] if general else []) + [(0, load), (2, store)]))
            finish_stores(sp, stored_x)
            finish_stores(sp, stored_h)

        @block.gpsimd
        def _(pool):
            def copy(i, par, half):
                wait_past(pool, S["acc"], i - 1)
                copy_columns(k, i, par).then_inc(S["copied"], 1)

            def root(i, par, half):
                pool.wait_ge(S["var"], i + 1)
                nc.gpsimd.tensor_tensor(k.st[par][:, 9:10], k.st[par][:, 8:9], k.mhalf[:, 0:1],
                                        ALU.pow).then_inc(S["rstd"], 1)

            pipelined(pool, [(0, copy), (2, root)])

        @block.tensor
        def _(pe):
            def run(general):
                def agg(i, par, half):
                    pe.wait_ge(S["copied"], i + 1)
                    wait_past(pe, S["t"], i - 1)
                    aggregate(k, pe, par, half, k.pairA, extra_ready if general else None).then_inc(S["acc"], 1)

                def turn_both(i, par, half):
                    pe.wait_ge(S["t"], i + 1)
                    pe.wait_ge(loaded[par], 32 * (half + 1))
                    wait_past(pe, S["tT"], i - 1)
                    for c in range(KC):
                        out = k.ps[0:128, 2 + par, c * P:(c + 1) * P]
                        pe.matmul(out, k.rel[:, 128 * c:128 * (c + 1)],
                                  k.CT[:, bass.ds(i, 1), :].rearrange("r o p -> r (o p)"), start=True, stop=False)
                        pe.matmul(out, k.t[par][:, 128 * c:128 * (c + 1)], k.ident[:, 0:P], start=False, stop=True)
                    turn(k, pe, S, i, par, 2 + par, 2 * P, k.hin[par], None).then_inc(S["turned"], 1)

                def dense(i, par, half):
                    pe.wait_ge(S["tT"], i + 1)
                    wait_past(pe, S["u"], i - 1)
                    red, h = k.tT[par][:, 0:KC, :], k.tT[par][:, KC:2 * KC, :]
                    rz, new = k.ps[0:P, 4 + 2 * par, :], k.ps[0:P, 5 + 2 * par, :]
                    for n, (x, w) in enumerate(((red, k.wih), (h, k.whh))):
                        for c in range(KC):
                            pe.matmul(rz, x[:, c, :], w[:, c, 0:2 * FEAT], start=(n + c == 0), stop=(n + c == 2))
                    product(k, pe, new[:, 0:FEAT], red, k.wih[:, :, 2 * FEAT:3 * FEAT])
                    product(k, pe, new[:, FEAT:2 * FEAT], h, k.whh[:, :, 2 * FEAT:3 * FEAT]).then_inc(S["product"], 1)

                pipelined(pe, [(0, agg), (1, turn_both), (2, dense)])

            either(pe, k, run)

        @block.scalar
        def _(act):
            s = nc.scalar

            def scale_high(i, par, half):
                act.wait_ge(S["acc"], i + 1)
                wait_past(act, S["t"], i - 1)
                s.activation(k.aw[par][:, :], k.ps[0:P, par, 0:FEAT], ACT.Copy, scale=CNT / UP).then_inc(S["aw"], 1)

            def tT_out(i, par, half):
                act.wait_ge(S["turned"], i + 1)
                wait_past(act, S["product"], i - 1)
                s.copy(k.tT[par][:, :, :], k.ps[0:128, 2 + par, 0:2 * KC * P]
                       .rearrange("f (c p) -> f c p", p=P)).then_inc(S["tT"], 1)

            def gates(i, par, half):
                act.wait_ge(S["rz"], i + 1)
                s.activation(k.rz[:, :], k.rz[:, :], ACT.Sigmoid).then_inc(S["gates"], 1)
                act.wait_ge(S["pre"], i + 1)
                s.activation(k.new[:, :], k.new[:, :], ACT.Tanh).then_inc(S["new"], 1)
                act.wait_ge(S["nmr"], i + 1)
                wait_slot(act, stored_h, par, half)
                s.activation(k.ho[par][:, :], k.xo[par][:, :], ACT.Relu, bias=k.st[par][:, 10:11],
                             scale=k.st[par][:, 11:12]).then_inc(S["h"], 1)
                act.wait_ge(S["h"], i + 1)
                split_scaled(k, s, k.pairB, i, k.ho[par], 1.0).then_inc(S["hi"], 1)

            pipelined(act, [(0, scale_high), (1, tT_out), (2, gates)])

        @block.vector
        def _(dve):
            v = nc.vector
            stt = v.scalar_tensor_tensor
            own = Chain(dve, S["own"], 7)

            def combine(i, par, half):
                dve.wait_ge(S["aw"], i + 1)
                wait_past(dve, S["turned"], i - 1)
                stt(out=k.t[par][:, :], in0=k.ps[0:P, par, FEAT:2 * FEAT], scalar=CNT / UP, in1=k.aw[par][:, :],
                    op0=ALU.mult, op1=ALU.add).then_inc(S["t"], 1)

            def cell(i, par, half):
                own.tile(i)
                rz, new = k.ps[0:P, 4 + 2 * par, :], k.ps[0:P, 5 + 2 * par, :]
                x, h, st = k.xo[par], k.hin[par], k.st[par]
                r, z = k.rz[:, 0:FEAT], k.rz[:, FEAT:2 * FEAT]
                dve.wait_ge(S["product"], i + 1)
                v.tensor_tensor(k.rz[:, :], rz, k.bi[:, 0:2 * FEAT], ALU.add).then_inc(S["rz"], 1)
                v.tensor_tensor(k.tmp[:, :], new[:, 0:FEAT], k.bi[:, 2 * FEAT:3 * FEAT], ALU.add)
                v.tensor_tensor(k.new[:, :], new[:, FEAT:2 * FEAT], k.bhn[:, :], ALU.add).then_inc(S["u"], 1)
                dve.wait_ge(S["u"], i + 1)
                dve.wait_ge(S["gates"], i + 1)
                own.link(v.tensor_tensor(k.new[:, :], k.new[:, :], r, ALU.mult))
                v.tensor_tensor(k.new[:, :], k.new[:, :], k.tmp[:, :], ALU.add).then_inc(S["pre"], 1)
                dve.wait_ge(S["new"], i + 1)
                own.link(v.tensor_tensor(k.tmp[:, :], h[:, :], k.new[:, :], ALU.subtract))
                own.link(v.tensor_tensor(k.tmp[:, :], k.tmp[:, :], z, ALU.mult))
                own.link(v.tensor_tensor(k.tmp[:, :], k.tmp[:, :], k.new[:, :], ALU.add))
                wait_slot(dve, stored_x, par, half)
                v.tensor_tensor(x[:, :], k.tmp[:, :], k.xin[par][:, :], ALU.add).then_inc(S["x"], 1)
                dve.wait_ge(S["x"], i + 1)
                own.link(v.bn_stats(st[:, 0:6], x[:, :]))
                settle(dve, k)
                own.link(v.bn_aggr(st[:, 6:8], st[:, 0:6]))
                v.tensor_scalar(st[:, 8:9], st[:, 7:8], EPS, None, ALU.add).then_inc(S["var"], 1)
                dve.wait_ge(S["rstd"], i + 1)
                own.link(v.tensor_tensor(st[:, 11:12], st[:, 9:10], k.dinvu[:, bass.ds(i, 1)], ALU.mult))
                v.tensor_scalar(st[:, 10:11], st[:, 6:7], st[:, 11:12], -1.0, ALU.mult, ALU.mult).then_inc(S["nmr"], 1)
                dve.wait_ge(S["hi"], i + 1)
                v.tensor_tensor(k.pairB[:, bass.ds(i, 1), FEAT:2 * FEAT], k.ho[par][:, :].unsqueeze(1),
                                k.pairB[:, bass.ds(i, 1), 0:FEAT], ALU.subtract).then_inc(S["lo"], 1)

            pipelined(dve, [(0, combine), (2, cell)])


def copy_columns(k, i, par):
    return k.nc.gpsimd.tensor_copy(k.blk[par][:, :].bitcast(U32).rearrange("p (j w) -> p j w", w=WORDS),
                                   k.adj[:, :, :].bitcast(U32)[:, :, bass.ds(i * WORDS, WORDS)])


def gcn(k):
    nc, d = k.nc, k.d
    S = {n: k.sem("gcn_" + n) for n in ("copied", "acc", "aw", "t", "turned", "tT", "product", "u", "x", "y", "var",
                                        "rstd", "nmr", "h", "turned2", "tT2", "product2", "var2", "rstd2", "nmr2",
                                        "z", "own", "own2", "own3")}
    extra_ready = k.sems("gcn_extra")
    loaded, loaded_x, stored = k.sems("gcn_loaded"), k.sems("gcn_loaded_x"), k.sems("gcn_stored")
    with nc.Block() as block:

        @block.sync
        def _(sp):
            def load_s(i, par, half):
                wait_past(sp, S["t"], i - 1)
                settle(sp, k)
                sp.dma_start(k.hin[par][:, :], rows(d["s2"], i)).then_inc(loaded[par], 16)

            def load_x(i, par, half):
                wait_past(sp, S["x"], i - 1)
                settle(sp, k)
                sp.dma_start(k.xin[par][:, :], rows(d["x2"], i)).then_inc(loaded_x[par], 16)

            def store(i, par, half):
                sp.wait_ge(S["z"], i + 1)
                settle(sp, k)
                sp.dma_start(rows(d["z"], i), k.z[par][:, :]).then_inc(stored[par], 16)
                sp.dma_start(rows(d["alpha_l"], i), k.z[par][:, FEAT + HEADS:ZW]).then_inc(stored[par], 16)

            either(sp, k, lambda general: pipelined(sp, (
                [(0, extra_loads(k, sp, S["acc"], extra_ready))] if general else []) + [(0, load_s), (1, load_x), (5, store)]))
            for par in range(2):
                sp.wait_ge(stored[par], 32 * ((TILES + 1 - par) // 2))

        @block.gpsimd
        def _(pool):
            def copy(i, par, half):
                wait_past(pool, S["acc"], i - 1)
                copy_columns(k, i, par).then_inc(S["copied"], 1)

            def root(i, par, half):
                pool.wait_ge(S["var"], i + 1)
                nc.gpsimd.tensor_tensor(k.st[par][:, 9:10], k.st[par][:, 8:9], k.mhalf[:, 0:1],
                                        ALU.pow).then_inc(S["rstd"], 1)
                pool.wait_ge(S["var2"], i + 1)
                nc.gpsimd.tensor_tensor(k.st2[par][:, 9:10], k.st2[par][:, 8:9], k.mhalf[:, 0:1],
                                        ALU.pow).then_inc(S["rstd2"], 1)

            pipelined(pool, [(0, copy), (2, root)])

        @block.tensor
        def _(pe):
            def run(general):
                def agg(i, par, half):
                    pe.wait_ge(S["copied"], i + 1)
                    wait_past(pe, S["t"], i - 1)
                    aggregate(k, pe, par, half, k.pairB, extra_ready if general else None).then_inc(S["acc"], 1)

                def turn_t(i, par, half):
                    pe.wait_ge(S["t"], i + 1)
                    wait_past(pe, S["tT"], i)
                    turn(k, pe, S, i, par, 2, 0, k.t[par], None).then_inc(S["turned"], 1)

                def dense(i, par, half):
                    pe.wait_ge(S["tT"], i + 1)
                    wait_past(pe, S["u"], i)
                    product(k, pe, k.ps[0:P, 3, 0:FEAT], k.tT[par], k.Wg).then_inc(S["product"], 1)

                def turn_h(i, par, half):
                    pe.wait_ge(S["h"], i + 1)
                    wait_past(pe, S["tT2"], i)
                    turn(k, pe, S, i, par, 4, 0, k.ho[par], None).then_inc(S["turned2"], 1)

                def dense_z(i, par, half):
                    pe.wait_ge(S["tT2"], i + 1)
                    wait_past(pe, S["z"], i - 1)
                    product(k, pe, k.ps[0:P, 5 + par, 0:ZW], k.tT[par][:, KC:2 * KC, :], k.Wz).then_inc(S["product2"], 1)

                pipelined(pe, [(0, agg), (1, turn_t), (2, dense), (4, turn_h), (5, dense_z)])

            either(pe, k, run)

        @block.scalar
        def _(act):
            s = nc.scalar

            def scale_high(i, par, half):
                act.wait_ge(S["acc"], i + 1)
                wait_past(act, S["t"], i - 1)
                s.activation(k.aw[par][:, :], k.ps[0:P, par, 0:FEAT], ACT.Copy,
                             scale=k.dinvs[:, bass.ds(i, 1)]).then_inc(S["aw"], 1)

            def tT_out(i, par, half):
                act.wait_ge(S["turned"], i + 1)
                wait_past(act, S["product"], i - 1)
                s.copy(k.tT[par][:, 0:KC, :], k.ps[0:128, 2, 0:2 * P]
                       .rearrange("f (c p) -> f c p", p=P)).then_inc(S["tT"], 1)

            def norms(i, par, half):
                act.wait_ge(S["nmr"], i + 1)
                s.activation(k.new[:, :], k.tmp[:, :], ACT.Identity, bias=k.st[par][:, 10:11],
                             scale=k.st[par][:, 9:10]).then_inc(S["y"], 1)
                act.wait_ge(S["nmr2"], i + 1)
                wait_past(act, S["turned2"], i - 1)
                s.activation(k.ho[par][:, :].unsqueeze(1), k.x3[:, bass.ds(i, 1), :], ACT.Relu, bias=k.st2[par][:, 10:11],
                             scale=k.st2[par][:, 9:10]).then_inc(S["h"], 1)

            def tT2_out(i, par, half):
                act.wait_ge(S["turned2"], i + 1)
                wait_past(act, S["product2"], i - 1)
                s.copy(k.tT[par][:, KC:2 * KC, :], k.ps[0:128, 4, 0:2 * P]
                       .rearrange("f (c p) -> f c p", p=P)).then_inc(S["tT2"], 1)

            def z_out(i, par, half):
                act.wait_ge(S["product2"], i + 1)
                if not isinstance(half, int) or half > 0:
                    act.wait_ge(stored[par], 32 * half)
                s.copy(k.z[par][:, :], k.ps[0:P, 5 + par, 0:ZW]).then_inc(S["z"], 1)

            pipelined(act, [(0, scale_high), (1, tT_out), (2, norms), (4, tT2_out), (5, z_out)])

        @block.vector
        def _(dve):
            v = nc.vector
            stt = v.scalar_tensor_tensor
            own, own2 = Chain(dve, S["own"], 1), Chain(dve, S["own2"], 6)

            def combine(i, par, half):
                own.tile(i)
                dve.wait_ge(loaded[par], 16 * (half + 1))
                dve.wait_ge(S["aw"], i + 1)
                wait_past(dve, S["turned"], i - 1)
                wait_past(dve, S["t"], i)
                own.link(stt(out=k.sum[:, :], in0=k.hin[par][:, :], scalar=1.0 / CNT, in1=k.ps[0:P, par, FEAT:2 * FEAT],
                             op0=ALU.mult, op1=ALU.add))
                stt(out=k.t[par][:, :], in0=k.sum[:, :], scalar=k.dinvs[:, bass.ds(i, 1)], in1=k.aw[par][:, :],
                    op0=ALU.mult, op1=ALU.add).then_inc(S["t"], 1)

            def norms(i, par, half):
                own2.tile(i)
                st, st2, c = k.st[par], k.st2[par], k.tmp
                dve.wait_ge(S["product"], i + 1)
                v.tensor_tensor(c[:, :], k.ps[0:P, 3, 0:FEAT], k.bg[:, :], ALU.add).then_inc(S["u"], 1)
                dve.wait_ge(S["u"], i + 1)
                own2.link(v.bn_stats(st[:, 0:6], c[:, :]))
                settle(dve, k)
                own2.link(v.bn_aggr(st[:, 6:8], st[:, 0:6]))
                v.tensor_scalar(st[:, 8:9], st[:, 7:8], EPS, None, ALU.add).then_inc(S["var"], 1)
                dve.wait_ge(S["rstd"], i + 1)
                v.tensor_scalar(st[:, 10:11], st[:, 6:7], st[:, 9:10], -1.0, ALU.mult, ALU.mult).then_inc(S["nmr"], 1)
                dve.wait_ge(S["y"], i + 1)
                own2.link(v.tensor_tensor(k.new[:, :], k.new[:, :], k.gamma[:, :], ALU.mult))
                own2.link(v.tensor_tensor(k.new[:, :], k.new[:, :], k.beta[:, :], ALU.add))
                dve.wait_ge(loaded_x[par], 16 * (half + 1))
                stt(out=k.x3[:, bass.ds(i, 1), :], in0=k.new[:, :].unsqueeze(1), scalar=0.0, in1=k.xin[par][:, :].unsqueeze(1),
                    op0=ALU.max, op1=ALU.add).then_inc(S["x"], 1)
                dve.wait_ge(S["x"], i + 1)
                settle(dve, k)
                own2.link(v.bn_stats(st2[:, 0:6], k.x3[:, bass.ds(i, 1), :].rearrange("p o f -> p (o f)")))
                settle(dve, k)
                own2.link(v.bn_aggr(st2[:, 6:8], st2[:, 0:6]))
                v.tensor_scalar(st2[:, 8:9], st2[:, 7:8], EPS, None, ALU.add).then_inc(S["var2"], 1)
                dve.wait_ge(S["rstd2"], i + 1)
                v.tensor_scalar(st2[:, 10:11], st2[:, 6:7], st2[:, 9:10], -1.0, ALU.mult, ALU.mult).then_inc(S["nmr2"], 1)

            pipelined(dve, [(0, combine), (2, norms)])


def attention(k):
    nc, d = k.nc, k.d
    PARTS, PT = 5, TILES // 5
    indexed, gathered, stored = k.sem("att_indexed"), [k.sem(f"att_gathered{n}") for n in range(PARTS)], k.sem("att_stored")
    shifted, raised, done, ok = (k.sem("att_" + n) for n in ("shifted", "raised", "done", "ok"))
    idx = k.st_i
    far = k.adj[:, :, :].rearrange("p t c -> p (t c)")[:, 0:4 * TILES * ZW].bitcast(F32).rearrange("p (t z) -> p t z", z=ZW)
    prod = k.adj[:, :, :].rearrange("p t c -> p (t c)")[:, 4 * TILES * ZW:4 * TILES * ZW + 4 * PT * FEAT].bitcast(F32)
    al = k.al
    with nc.Block() as block:

        @block.gpsimd
        def _(pool):
            pool.wait_ge(indexed, 32)
            for i in range(TILES):
                for out, table, side in ((al[:, i, :], d["alpha_l"], 0), (far[:, i, :], d["z"], 1)):
                    nc.gpsimd.indirect_dma_start(out, None, table[:, :], bass.IndirectOffsetOnAxis(ap=idx[:, side, i:i + 1], axis=0)
                                                 ).then_inc(gathered[i // PT], 16)

        @block.sync
        def _(sp):
            sp.dma_start(idx[:, 0, :], d["srcT"][:, 0:TILES]).then_inc(indexed, 16)
            sp.dma_start(idx[:, 1, :], d["dstT"][:, 0:TILES]).then_inc(indexed, 16)
            for n in range(PARTS):
                sp.wait_ge(done, n + 1)
                settle(sp, k)
                sp.dma_start(d["out"][n * PT * P:(n + 1) * PT * P, :].rearrange("(t p) f -> p t f", p=P),
                             k.x3[:, n * PT:(n + 1) * PT, :]).then_inc(stored, 16)
            sp.wait_ge(stored, 16 * PARTS)

        @block.scalar
        def _(act):
            for n in range(PARTS):
                act.wait_ge(shifted, n + 1)
                a = al[:, n * PT:(n + 1) * PT, :]
                nc.scalar.activation(a, a, ACT.Exp).then_inc(raised, 1)

        @block.vector
        def _(dve):
            v = nc.vector
            own = Chain(dve, ok, 100).tile(0)
            for n in range(PARTS):
                tiles = slice(n * PT, (n + 1) * PT)
                a, z, x = al[:, tiles, :], far[:, tiles, :], k.x3[:, tiles, :]
                most = k.st[0][:, 0:PT]
                dve.wait_ge(gathered[n], 32 * PT)
                own.link(v.tensor_tensor(a, a, z[:, :, FEAT:FEAT + HEADS], ALU.add))
                own.link(v.scalar_tensor_tensor(out=a, in0=a, scalar=0.01, in1=a, op0=ALU.mult, op1=ALU.max))
                own.link(v.tensor_reduce(most, a, AX.X, ALU.max))
                v.tensor_tensor(a, a, most.unsqueeze(2).to_broadcast([P, PT, HEADS]), ALU.subtract).then_inc(shifted, 1)
                dve.wait_ge(raised, n + 1)
                own.link(v.tensor_reduce(most, a, AX.X, ALU.add))
                own.link(v.reciprocal(most, most))
                own.link(v.tensor_tensor(a, a, most.unsqueeze(2).to_broadcast([P, PT, HEADS]), ALU.mult))
                own.link(v.tensor_tensor(prod.rearrange("p (t h c) -> p t h c", h=HEADS, c=DH),
                                         z[:, :, 0:FEAT].rearrange("p t (h c) -> p t h c", h=HEADS),
                                         a.unsqueeze(3).to_broadcast([P, PT, HEADS, DH]), ALU.mult))
                total = k.total[:, :].rearrange("p (t c) -> p t c", c=DH)
                own.link(v.tensor_reduce(total, prod.rearrange("p (t h c) -> p t c h", h=HEADS, c=DH), AX.X, ALU.add))
                v.tensor_tensor(x.rearrange("p t (h c) -> p t h c", h=HEADS), x.rearrange("p t (h c) -> p t h c", h=HEADS),
                                total.unsqueeze(2).to_broadcast([P, PT, HEADS, DH]), ALU.add).then_inc(done, 1)


def phases(k):
    d = k.d
    for phase in (
            setup, build, degrees,
            lambda k: edge_sums(k, "e0", d["h0"], "dstT", "srcT", UP / CNT),
            lambda k: mean_by_destination(k, "mean1", k.pairA, k.pairB, d["m1"], False),
            lambda k: edge_sums(k, "e1", d["m1"], "srcT", "dstT", 1.0 / CNT, True),
            lambda k: scatter_mean(k, "back1", k.pairB, True),
            lambda k: edge_sums(k, "e2", d["g"], "dstT", "srcT", 1.0 / CNT),
            lambda k: mean_by_destination(k, "mean2", k.pairA, k.pairB, d["m2"], True),
            lambda k: edge_sums(k, "e3", d["m2"], "srcT", "dstT", 1.0 / CNT),
            lambda k: scatter_mean(k, "back2", k.pairB, False),
            lambda k: edge_sums(k, "e4", d["h1"], "dstT", "srcT", UP / CNT),
            gru,
            lambda k: edge_sums(k, "e5", d["s2"], "dstT", "srcT", 1.0 / CNT),
            gcn, attention):
        phase(k)
        k.end_phase()


def program(nc, d):
    with ExitStack() as ctx:
        for name in ("h0", "m1", "g", "m2", "h1", "s2", "x1", "x2", "extra"):
            d[name] = nc.dram_tensor("t_" + name, (NODES, FEAT), F32).ap()
        d["adjT"] = nc.dram_tensor("t_adjT", (TILES, P, ROW // 4), U32).ap()
        d["z"] = nc.dram_tensor("t_z", (NODES, ZW), F32).ap()
        d["alpha_l"] = nc.dram_tensor("t_alpha_l", (NODES, HEADS), F32).ap()
        k = Kernel(nc, ctx, d)
        phases(k)


INPUTS = {"x": "x", "W1": "L0_gnn_W1", "b1": "L0_gnn_b1", "W2": "L0_gnn_W2", "b2": "L0_gnn_b2", "a": "L0_gnn_a",
          "relv": "L1_gnn_relvectors", "b_ih": "L1_gnn_b_ih", "b_hh": "L1_gnn_b_hh", "bg": "L2_gnn_b",
          "gamma": "L2_gnn_gamma", "beta": "L2_gnn_beta", "weight": "L3_gnn_weight"}


def kernel(**inputs):
    import concourse.bacc as _bacc
    import numpy as _np
    from concourse.bass_utils import run_bass_kernel_spmd as _run

    given = {name: _np.asarray(inputs[source]) for name, source in INPUTS.items()}
    for name, source in (("srcT", "src"), ("dstT", "dst"), ("relT", "edge_type_16")):
        given[name] = _np.asarray(inputs[source]).reshape(CHUNKS, P).T
    for name, source in (("w_ihT", "L1_gnn_w_ih"), ("w_hhT", "L1_gnn_w_hh"), ("WgT", "L2_gnn_W")):
        given[name] = _np.asarray(inputs[source]).T
    for name, source in (("attn_l", "L3_gnn_attn_l"), ("attn_r", "L3_gnn_attn_r")):
        given[name] = _np.asarray(inputs[source]).reshape(FEAT)
    nc = _bacc.Bacc("TRN2", target_bir_lowering=False, num_devices=1)
    arrays, d = {}, {}
    for name, a in given.items():
        arrays["in_" + name] = _np.ascontiguousarray(a)
        d[name] = nc.dram_tensor("in_" + name, a.shape, mybir.dt.from_np(a.dtype), kind="ExternalInput").ap()
    d["out"] = nc.dram_tensor("out", (NODES, FEAT), F32, kind="ExternalOutput").ap()
    program(nc, d)
    r = _run(nc, [arrays], core_ids=[0])
    return r.results[0]["out"]
```

```python
from contextlib import ExitStack

import concourse.bass as bass
from concourse import mybir

F32, BF16, F16 = mybir.dt.float32, mybir.dt.bfloat16, mybir.dt.float16
F8, I32, U32 = mybir.dt.float8e4, mybir.dt.int32, mybir.dt.uint32
ALU = mybir.AluOpType
ACT = mybir.ActivationFunctionType
AX = mybir.AxisListType

NODES, EDGES, FEAT, RELS, HEADS = 3125, 50000, 256, 16, 4
P = 125
TILES = NODES // P
CHUNKS = EDGES // P
PITCH = 128
ROW = TILES * PITCH
WORDS = PITCH // 4
WIN = 25
WPT = P // WIN
WINDOWS = NODES // WIN
KEYS = TILES * WIN
HALF_A = 13
QUAD = 4
KW = 640
PADDED = CHUNKS + 2 * QUAD
DH = FEAT // HEADS
KC = FEAT // 128
ZW = FEAT + 2 * HEADS
UP = 2048.0
CNT = 8.0
EPS = 1e-5


def pipelined(eng, stages):
    lag = max(l for l, _ in stages)
    first = (lag + 3) // 2 * 2

    def step(k, half, par):
        for l, fn in stages:
            if isinstance(k, int) and not 0 <= k - l < TILES:
                continue
            fn(k - l, (par - l) % 2, half + (par - l) // 2)

    for k in range(first):
        step(k, k // 2, k % 2)
    with eng.Fori(first // 2, TILES // 2) as r:
        step(2 * r, r, 0)
        step(2 * r + 1, r, 1)
    for k in range(TILES - 1, TILES + lag):
        step(k, k // 2, k % 2)


def wait_past(eng, sem, value):
    if not (isinstance(value, int) and value <= 0):
        eng.wait_ge(sem, value)


def settle(eng, k):
    eng.sem_inc(k.noted, 1)


class Chain:

    def __init__(self, eng, sem, per_tile):
        self.eng, self.sem, self.per_tile, self.n = eng, sem, per_tile, 0

    def tile(self, i):
        assert self.n in (0, self.per_tile)
        self.base, self.n = i * self.per_tile, 0
        return self

    def link(self, ins):
        self.n += 1
        assert self.n <= self.per_tile
        ins.then_inc(self.sem, 1)
        self.eng.wait_ge(self.sem, self.base + self.n)
        return self


class Kernel:

    def __init__(self, nc, ctx, d):
        self.nc, self.ctx, self.d = nc, ctx, d
        self.phase_sems = []
        self.noted = nc.alloc_semaphore(name="noted")
        sb = self.sb
        self.ps = ctx.enter_context(nc.psum_tensor("ps", [128, 8, 512], F32))
        self.adj = sb("adj", [P, TILES, ROW], F8)
        self.pairA = sb("pairA", [P, TILES, 2 * FEAT], F16)
        self.pairB = sb("pairB", [P, TILES, 2 * FEAT], F16)
        self.blk = [sb(f"blk{i}", [P, ROW], F8) for i in range(2)]
        self.row = [sb(f"row{i}", [P, ROW], F8) for i in range(2)]
        self.xin = [sb(f"xin{i}", [P, FEAT], F32) for i in range(2)]
        self.ho = [sb(f"ho{i}", [P, FEAT], F32) for i in range(2)]
        self.work = sb("work", [128, 8 * FEAT + 2 * 2 * KC * P], F32)
        tile = [self.work[0:P, FEAT * n:FEAT * (n + 1)] for n in range(8)]
        self.hin, self.aw, self.t, self.xo = tile[0:2], tile[2:4], tile[4:6], tile[6:8]
        self.tT = [self.work[:, 8 * FEAT + n * 2 * KC * P:8 * FEAT + (n + 1) * 2 * KC * P]
                   .rearrange("f (c p) -> f c p", p=P) for n in range(2)]
        self.st = [sb(f"st{i}", [P, 16], F32) for i in range(2)]
        self.W1 = sb("W1", [128, KC, FEAT], F32)
        self.W2 = sb("W2", [128, KC, FEAT], F32)
        self.wih = sb("wih", [128, KC, 3 * FEAT], F32)
        self.whh = sb("whh", [128, KC, 3 * FEAT], F32)
        self.Wg = sb("Wg", [128, KC, FEAT], F32)
        self.Wz = sb("Wz", [128, KC, ZW], F32)
        self.b1 = sb("b1", [P, FEAT], F32)
        self.b2 = sb("b2", [P, FEAT], F32)
        self.bg = sb("bg", [P, FEAT], F32)
        self.gamma = sb("gamma", [P, FEAT], F32)
        self.beta = sb("beta", [P, FEAT], F32)
        self.bi = sb("bi", [P, 3 * FEAT], F32)
        self.bhn = sb("bhn", [P, FEAT], F32)
        self.rel = sb("rel", [RELS, FEAT], F32)
        self.ident = sb("ident", [P, 128], F32)
        self.identb = sb("identb", [P, 128], BF16)
        self.ones = sb("ones", [128, P], F32)
        self.mhalf = sb("mhalf", [P, 32], F32)
        self.slope = sb("slope", [P, 1], F32)
        self.gslope = sb("gslope", [P, 1], F32)
        self.gscale = sb("gscale", [P, 1], F32)
        self.gunscale = sb("gunscale", [P, 1], F32)
        self.CT = sb("CT", [RELS, TILES, P], F32)
        self.indeg = sb("indeg", [P, 32], F32)
        self.odeg8 = sb("odeg8", [P, 32], F32)
        self.rsB = sb("rsB", [P, 32], F32)
        self.rsD = sb("rsD", [P, 32], F32)
        self.rsD4 = sb("rsD4", [P, 32], F32)
        self.dinv = sb("dinv", [P, 32], F32)
        self.dinvs = sb("dinvs", [P, 32], F32)
        self.dinvu = sb("dinvu", [P, 32], F32)
        self.st2 = [sb(f"st2{i}", [P, 16], F32) for i in range(2)]
        self.st_i = sb("st_i", [P, 2, TILES], I32)
        self.al = sb("al", [P, TILES, HEADS], F32)
        self.table = sb("table", [1, 3 * 128], I32)
        self.flag = sb("flag", [1, 1], I32)
        self.extra = [sb(f"extra{i}", [P, FEAT], F32) for i in range(2)]
        self.junk = self.whh[0:P, :, :].rearrange("f c n -> f (c n)")[:, 0:ROW // 4].bitcast(F8)
        rows_f = [r[:, :].bitcast(F32) for r in self.row]
        self.sum = rows_f[1][:, FEAT:2 * FEAT]
        self.z = [rows_f[0][:, 0:ZW], rows_f[1][:, 2 * FEAT:2 * FEAT + ZW]]
        self.total = rows_f[0][:, 0:5 * DH]
        self.x3 = self.pairA[:, :, :].bitcast(F32)
        flat = self.pairB[:, :, :].rearrange("p t f -> p (t f)")
        self.keys = flat[:, 0:8 * PADDED].bitcast(F32).rearrange("p (c k) -> p c k", k=4)
        self.iota_keys = self.row[1][:, 0:2 * KW].bitcast(F16)
        self.iota_lo = self.row[1][:, 2 * KW:2 * KW + 512].bitcast(F32)
        self.win_off = self.row[1][:, 2 * KW + 512:2 * KW + 1024].bitcast(F32)
        spare = self.work[0:P, :].bitcast(BF16)
        self.hot_keys = ([flat[:, 8 * PADDED + n * QUAD * KW:8 * PADDED + (n + 1) * QUAD * KW].bitcast(BF16) for n in range(3)]
                         + [spare[:, 0:QUAD * KW]])
        self.hot_keys = [h.rearrange("p (u n) -> p u n", u=QUAD) for h in self.hot_keys]
        spare = spare[:, QUAD * KW:]
        self.hot_lo = [spare[:, 512 * n:512 * (n + 1)].rearrange("p (u n) -> p u n", u=QUAD) for n in range(4)]
        spare = spare[:, 4 * 512:]
        self.hot_rel = [spare[:, 208 * n:208 * (n + 1)].rearrange("p (u k n) -> p u k n", u=QUAD, k=2) for n in range(4)]
        spare = spare[:, 4 * 208:]
        self.quad_hi = [spare[:, 8 * n:8 * (n + 1)].bitcast(F32) for n in range(4)]
        self.quad_low = [spare[:, 32 + 16 * n:32 + 16 * (n + 1)].bitcast(F16).rearrange("p (u k) -> p u k", k=4)
                         for n in range(4)]
        self.over = self.row[0][:, :].bitcast(U32)

    def sb(self, name, shape, dt):
        return self.ctx.enter_context(self.nc.sbuf_tensor(name, shape, dt))

    def sem(self, name):
        self.phase_sems.append(self.nc.alloc_semaphore(name=name))
        return self.phase_sems[-1]

    def end_phase(self):
        for s in self.phase_sems:
            self.nc.sync.sem_clear(s)
            self.nc.release_semaphore(s)
        self.phase_sems = []
        self.nc.all_engine_barrier()

    def sems(self, name):
        return [self.sem(name + "0"), self.sem(name + "1")]


def rows(ap, i):
    return ap[bass.ds(i * P, P), :]


def either(eng, k, run):
    general = eng.value_load(k.flag[0:1, 0:1], min_val=0, max_val=1)
    with eng.If(general > 0):
        run(True)
    with eng.Else():
        run(False)


def edge_sums(k, name, x, key, other, value, outdegree=False):
    nc, d = k.nc, k.d
    DEEP = 4
    loaded = [k.sem(f"{name}_indexed{m}") for m in range(DEEP)]
    gathered = [nc.alloc_semaphore(name=f"{name}_gathered{m}") for m in range(DEEP)]
    made, hot, summed, out_ready, stored, ok = (k.sem(f"{name}_{n}") for n in (
        "made", "hot", "summed", "out", "stored", "ok"))
    iota, offset, zero = k.work[0:P, 0:128], k.work[0:P, 128:160], k.work[0:P, 256:512]
    ends = [k.work[0:P, 160 + 2 * n:162 + 2 * n].bitcast(I32) for n in range(DEEP)]
    keyf = [k.work[0:P, 160 + 2 * DEEP + n:161 + 2 * DEEP + n] for n in range(DEEP)]
    xg = [k.work[0:P, 512 + FEAT * n:512 + FEAT * (n + 1)] for n in range(DEEP)]
    oh = [k.work[0:P, 512 + DEEP * FEAT + 128 * n:512 + DEEP * FEAT + 128 * n + P] for n in range(DEEP)]

    with nc.Block() as block:

        @block.sync
        def _(sp):
            def run(general):
                if not general:
                    return
                with sp.Fori(0, TILES) as i:
                    with sp.Fori(0, CHUNKS // DEEP) as h:
                        for slot in range(DEEP):
                            c = DEEP * h + slot
                            sp.wait_ge(summed, CHUNKS * i + c + 1)
                            settle(sp, k)
                            sp.dma_start(ends[slot][:, 0:1], d[key][:, bass.ds(c, 1)], allow_slow_non_contiguous=True).then_inc(loaded[slot], 16)
                            sp.dma_start(ends[slot][:, 1:2], d[other][:, bass.ds(c, 1)], allow_slow_non_contiguous=True).then_inc(loaded[slot], 16)
                    sp.wait_ge(out_ready, i + 2)
                    settle(sp, k)
                    sp.dma_start(rows(d["extra"], i), k.extra[0][:, :]).then_inc(stored, 16)
                sp.wait_ge(stored, 16 * TILES + 1)

            either(sp, k, run)

        @block.gpsimd
        def _(pool):
            def run(general):
                if not general:
                    return
                g = nc.gpsimd
                g.iota(iota, pattern=[[1, 128]], base=0, channel_multiplier=0, allow_small_or_imprecise_dtypes=True)
                g.iota(offset, pattern=[[-P, 32]], base=0, channel_multiplier=0, allow_small_or_imprecise_dtypes=True)
                g.memset(zero, 0.0).then_inc(made, 1)
                with pool.Fori(0, TILES * CHUNKS // DEEP) as h:
                    for slot in range(DEEP):
                        pool.wait_ge(loaded[slot], 32 * h + 32)
                        settle(pool, k)
                        g.indirect_dma_start(xg[slot], None, x[:, :], bass.IndirectOffsetOnAxis(ap=ends[slot][:, 1:2], axis=0)
                                             ).then_inc(gathered[slot], 16)

            either(pool, k, run)

        @block.vector
        def _(dve):
            def run(general):
                if not general:
                    return
                v = nc.vector
                dve.wait_ge(made, 1)
                with dve.Fori(0, TILES) as i:
                    with dve.Fori(0, CHUNKS // DEEP) as h:
                        for slot in range(DEEP):
                            dve.wait_ge(loaded[slot], 32 * (CHUNKS // DEEP * i + h + 1))
                            v.tensor_copy(keyf[slot], ends[slot][:, 0:1]).then_inc(ok, 1)
                            dve.wait_ge(ok, CHUNKS * i + DEEP * h + slot + 1)
                            settle(dve, k)
                            v.tensor_scalar(oh[slot], iota[:, 0:P], keyf[slot], offset[:, bass.ds(i, 1)],
                                            ALU.subtract, ALU.is_equal).then_inc(hot, 1)

            either(dve, k, run)

        @block.tensor
        def _(pe):
            def run(general):
                if not general:
                    return
                pe.wait_ge(made, 1)
                pe.sem_inc(summed, DEEP)
                with pe.Fori(0, TILES) as i:
                    pe.wait_ge(out_ready, i + 1)
                    pe.matmul(k.ps[0:P, 7, 0:FEAT], zero[:, 0:P], zero, start=True, stop=True, skip_group_check=True)
                    if outdegree:
                        pe.matmul(k.ps[0:P, 6, 0:1], zero[:, 0:P], k.ones[0:P, 0:1], start=True, stop=True,
                                  skip_group_check=True)
                    with pe.Fori(0, CHUNKS // DEEP) as h:
                        for slot in range(DEEP):
                            pe.wait_ge(gathered[slot], 16 * (CHUNKS // DEEP * i + h + 1))
                            pe.wait_ge(hot, CHUNKS * i + DEEP * h + slot + 1)
                            if outdegree:
                                pe.matmul(k.ps[0:P, 6, 0:1], oh[slot], k.ones[0:P, 0:1], start=False, stop=True,
                                          skip_group_check=True)
                            pe.matmul(k.ps[0:P, 7, 0:FEAT], oh[slot], xg[slot], start=False, stop=True,
                                      skip_group_check=True).then_inc(summed, 1)

            either(pe, k, run)

        @block.scalar
        def _(act):
            def run(general):
                if not general:
                    return
                act.sem_inc(stored, 1)
                act.sem_inc(out_ready, 1)
                with act.Fori(0, TILES) as i:
                    act.wait_ge(summed, CHUNKS * i + CHUNKS + DEEP)
                    act.wait_ge(stored, 16 * i + 1)
                    settle(act, k)
                    if outdegree:
                        nc.scalar.activation(k.odeg8[:, bass.ds(i, 1)], k.ps[0:P, 6, 0:1], ACT.Copy, scale=1.0 / CNT)
                    nc.scalar.activation(k.extra[0][:, :], k.ps[0:P, 7, 0:FEAT], ACT.Copy,
                                         scale=value).then_inc(out_ready, 1)

            either(act, k, run)


def setup(k):
    nc, d = k.nc, k.d
    loaded, edges, made, ok = k.sem("setup_loaded"), k.sem("setup_edges"), k.sem("setup_made"), k.sem("setup_ok")
    picked, turned, bound = k.sem("setup_picked"), k.sem("setup_turned"), k.sem("setup_bound")
    have_pick, have_count, have_abs = k.sem("setup_have_pick"), k.sem("setup_have_count"), k.sem("setup_have_abs")
    flat = k.pairA[:, :, :].rearrange("p t f -> p (t f)").bitcast(F32)
    part = [flat[:, CHUNKS * n:CHUNKS * (n + 1)] for n in range(12)]
    raw = flat[:, 0:3 * CHUNKS].bitcast(I32)
    srcf, dstf, relf, win, tile, _, junk, pick = part[3:11]
    bh = flat[:, 11 * CHUNKS:11 * CHUNKS + 3 * FEAT]
    before = flat[:, 11 * CHUNKS + 3 * FEAT:12 * CHUNKS + 3 * FEAT]
    beforef = flat[:, 12 * CHUNKS + 3 * FEAT:13 * CHUNKS + 3 * FEAT]
    pidx, thresh, count = k.st[0][:, 0:1], k.st[0][:, 1:2], k.st[0][:, 2:3]
    scratch = k.st[1]
    att = k.work[:, 0:2 * FEAT].rearrange("f (s n) -> f s n", s=2)
    prod = k.work[:, 2 * FEAT:4 * FEAT].rearrange("f (c n) -> f c n", c=KC)
    with nc.Block() as block:

        @block.sync
        def _(sp):
            for n, name in enumerate(("srcT", "dstT", "relT")):
                sp.dma_start(raw[:, CHUNKS * n:CHUNKS * (n + 1)], d[name][:, :]).then_inc(edges, 16)
            prev = before.bitcast(I32)
            sp.dma_start(prev[1:P, :], d["dstT"][0:P - 1, :]).then_inc(edges, 16)
            sp.dma_start(prev[0:1, 1:CHUNKS], d["dstT"][P - 1:P, 0:CHUNKS - 1]).then_inc(edges, 16)
            sp.dma_start(prev[0:1, 0:1], d["dstT"][0:1, 0:1]).then_inc(edges, 16)
            for c, name in enumerate(("attn_r", "attn_l")):
                sp.dma_start(att[:, c, :], d[name].partition_broadcast(128)).then_inc(loaded, 16)
            for sb, name in ((k.W1, "W1"), (k.W2, "W2"), (k.wih, "w_ihT"), (k.Wg, "WgT"),
                             (k.Wz[:, :, 0:FEAT], "weight")):
                sp.dma_start(sb[:, :, 0:FEAT * (3 if name[0:2] == "w_" else 1)],
                             d[name].rearrange("(c f) n -> f c n", f=128)).then_inc(loaded, 16)
            for sb, name in ((k.b1, "b1"), (k.b2, "b2"), (k.bg, "bg"), (k.gamma, "gamma"), (k.beta, "beta"),
                             (k.bi, "b_ih"), (bh, "b_hh"), (k.slope, "a")):
                sp.dma_start(sb[:, :], d[name].partition_broadcast(P)).then_inc(loaded, 16)
            sp.dma_start(k.rel[:, :], d["relv"][:, :]).then_inc(loaded, 16)

        @block.gpsimd
        def _(pool):
            g = nc.gpsimd
            g.memset(k.mhalf[:, :], -0.5)
            g.memset(k.ones[:, :], 1.0)
            g.iota(k.iota_keys, pattern=[[1, KW]], base=0, channel_multiplier=0, allow_small_or_imprecise_dtypes=True)
            g.iota(k.iota_lo, pattern=[[1, 128]], base=0, channel_multiplier=0, allow_small_or_imprecise_dtypes=True)
            g.iota(k.win_off, pattern=[[-P, 128]], base=0, channel_multiplier=0, allow_small_or_imprecise_dtypes=True)
            g.iota(pidx, pattern=[[0, 1]], base=0, channel_multiplier=1, allow_small_or_imprecise_dtypes=True)
            g.iota(thresh, pattern=[[0, 1]], base=0, channel_multiplier=WIN,
                   allow_small_or_imprecise_dtypes=True).then_inc(made, 1)

        @block.vector
        def _(dve):
            v = nc.vector
            stt = v.scalar_tensor_tensor
            own = Chain(dve, ok, 100).tile(0)
            v.memset(k.odeg8[:, :], 0.0)
            v.memset(k.keys[:, CHUNKS:PADDED, :], -1.0)
            v.memset(k.blk[0][:, :].bitcast(U32), 0)
            v.memset(k.blk[1][:, :].bitcast(U32), 0)
            v.memset(k.row[0][:, :].bitcast(U32), 0)
            dve.wait_ge(made, 1)
            own.link(v.tensor_scalar(k.ident[:, :], k.iota_lo, pidx, None, ALU.is_equal))
            v.tensor_copy(k.identb[:, :], k.ident[:, :])
            own.link(v.tensor_scalar(scratch[:, 0:1], pidx, float(P - 1), None, ALU.is_equal))
            own.link(v.tensor_scalar(pick[:, 0:WINDOWS], k.ones[0:P, :], scratch[:, 0:1], None, ALU.mult))
            dve.wait_ge(edges, 96)
            v.tensor_copy(beforef, before.bitcast(I32))
            v.tensor_copy(srcf, raw[:, 0:CHUNKS])
            v.tensor_copy(dstf, raw[:, CHUNKS:2 * CHUNKS])
            own.link(v.tensor_copy(relf, raw[:, 2 * CHUNKS:3 * CHUNKS]))
            own.link(v.tensor_tensor(beforef, beforef, dstf, ALU.is_gt))
            own.link(v.tensor_reduce(scratch[:, 4:5], beforef, AX.X, ALU.add))
            dve.sem_inc(have_pick, 1)

            def floor_div(out, x, by):
                own.link(v.tensor_scalar(out, x, 0.5, 1.0 / by, ALU.add, ALU.mult))
                own.link(v.tensor_scalar(out, out, -0.5, None, ALU.add))
                own.link(v.tensor_scalar(out, out, 12582912.0, None, ALU.add))
                own.link(v.tensor_scalar(out, out, -12582912.0, None, ALU.add))

            floor_div(win, dstf, WIN)
            floor_div(tile, srcf, P)
            lo_key, rel_key, hi_key, din = (k.keys[:, 0:CHUNKS, n] for n in range(4))
            own.link(stt(out=lo_key, in0=win, scalar=float(P), in1=srcf, op0=ALU.mult, op1=ALU.add))
            own.link(stt(out=lo_key, in0=tile, scalar=-float(P), in1=lo_key, op0=ALU.mult, op1=ALU.add))
            own.link(stt(out=rel_key, in0=win, scalar=float(P), in1=relf, op0=ALU.mult, op1=ALU.add))
            own.link(stt(out=din, in0=win, scalar=-float(WIN), in1=dstf, op0=ALU.mult, op1=ALU.add))
            own.link(stt(out=hi_key, in0=tile, scalar=float(WIN), in1=din, op0=ALU.mult, op1=ALU.add))
            dve.wait_ge(picked, 1)
            own.link(v.tensor_scalar(junk, k.ps[0:P, 0, 0:CHUNKS], thresh, 0.0, ALU.is_lt, ALU.add, accum_out=count))
            own.link(v.tensor_scalar(count, count, float(CHUNKS - 1), None, ALU.min))
            dve.sem_inc(have_count, 1)
            dve.wait_ge(loaded, 16 * 16)
            for side in range(2):
                for c in range(KC):
                    own.link(v.tensor_tensor(prod[:, c, :], k.Wz[:, c, 0:FEAT], att[:, side, :], ALU.mult))
                    own.link(v.tensor_reduce(k.Wz[:, c, FEAT + HEADS * side:FEAT + HEADS * (side + 1)],
                                             prod[:, c, :].rearrange("p (h n) -> p h n", n=DH), AX.X, ALU.add))
            own.link(stt(out=prod, in0=k.W1[:, :, :], scalar=-1.0, in1=k.W1[:, :, :], op0=ALU.mult, op1=ALU.max))
            dve.sem_inc(have_abs, 1)
            absb = junk[:, 0:FEAT]
            own.link(stt(out=absb, in0=k.b1[:, :], scalar=-1.0, in1=k.b1[:, :], op0=ALU.mult, op1=ALU.max))
            own.link(stt(out=scratch[:, 1:2], in0=k.slope[:, :], scalar=-1.0, in1=k.slope[:, :], op0=ALU.mult, op1=ALU.max))
            own.link(v.tensor_scalar(scratch[:, 1:2], scratch[:, 1:2], 1.0, None, ALU.max))
            dve.wait_ge(bound, 1)
            own.link(stt(out=absb, in0=k.ps[0:P, 2, 0:FEAT], scalar=16.0, in1=absb, op0=ALU.mult, op1=ALU.add))
            own.link(v.tensor_reduce(scratch[:, 0:1], absb, AX.X, ALU.max))
            own.link(v.tensor_scalar(scratch[:, 0:1], scratch[:, 0:1], scratch[:, 1:2], None, ALU.mult))
            own.link(v.tensor_scalar(scratch[:, 0:1], scratch[:, 0:1], 2.0 ** -60, None, ALU.max))
            own.link(v.tensor_scalar(scratch[:, 2:3].bitcast(I32), scratch[:, 0:1].bitcast(I32), 0x7F800000, None,
                                     ALU.bitwise_and))
            own.link(v.tensor_scalar(scratch[:, 3:4], scratch[:, 2:3], 2.0 ** -14, None, ALU.mult))
            own.link(v.reciprocal(k.gscale[:, :], scratch[:, 3:4]))
            own.link(v.tensor_scalar(k.gunscale[:, :], scratch[:, 3:4], CNT, None, ALU.mult))
            own.link(v.tensor_tensor(k.gslope[:, :], k.gscale[:, :], k.slope[:, :], ALU.mult))
            own.link(v.tensor_tensor(k.bi[:, 0:2 * FEAT], k.bi[:, 0:2 * FEAT], bh[:, 0:2 * FEAT], ALU.add))
            own.link(v.tensor_copy(k.bhn[:, :], bh[:, 2 * FEAT:3 * FEAT]))
            dve.wait_ge(turned, 1)
            some, none = scratch[0:1, 5:6], scratch[0:1, 6:7]
            first, last = junk[0:1, 0:WINDOWS], junk[0:1, 128:128 + WINDOWS]
            more, sums = junk[0:1, 256:256 + WINDOWS + 1], pick[0:1, 0:WINDOWS + 1]
            own.link(v.tensor_scalar(some, k.ps[0:1, 3, 0:1], 0.0, None, ALU.is_gt))
            own.link(v.tensor_scalar(none, some, -1.0, 1.0, ALU.mult, ALU.add))
            own.link(v.tensor_copy(first, k.ps[0:1, 1, 0:WINDOWS]))
            v.tensor_scalar(k.table[0:1, 0:WINDOWS], first, none, None, ALU.mult)
            own.link(v.memset(last[:, WINDOWS - 1:WINDOWS], CHUNKS - 1))
            own.link(v.tensor_copy(last[:, 0:WINDOWS - 1], first[:, 1:WINDOWS]))
            own.link(v.tensor_tensor(last, last, first, ALU.subtract))
            own.link(v.tensor_scalar(first, last, -1.0, float(CHUNKS - 1), ALU.mult, ALU.add))
            own.link(stt(out=last, in0=first, scalar=some, in1=last, op0=ALU.mult, op1=ALU.add))
            own.link(v.tensor_scalar(last, last, float(QUAD), None, ALU.add))
            own.link(v.memset(more[:, 0:1], 0.0))
            floor_div(more[:, 1:WINDOWS + 1], last, 2 * QUAD)
            own.link(v.tensor_copy(k.table[0:1, 128:128 + WINDOWS], more[:, 1:WINDOWS + 1]))
            shift = 1
            while shift <= WINDOWS:
                v.tensor_copy(sums[:, 0:shift], more[:, 0:shift])
                own.link(v.tensor_tensor(sums[:, shift:], more[:, shift:], more[:, 0:WINDOWS + 1 - shift], ALU.add))
                more, sums, shift = sums, more, 2 * shift
            own.link(v.tensor_copy(k.table[0:1, 256:256 + WINDOWS + 1], more))

        @block.tensor
        def _(pe):
            pe.wait_ge(have_pick, 1)
            pe.matmul(k.ps[0:P, 0, 0:CHUNKS], pick[:, 0:P], dstf, start=True, stop=True)
            pe.matmul(k.ps[0:1, 3, 0:1], scratch[:, 4:5], k.ones[0:P, 0:1], start=True, stop=True).then_inc(picked, 1)
            pe.wait_ge(have_count, 1)
            pe.matmul(k.ps[0:1, 1, 0:P], count, k.ident[:, 0:P], start=True, stop=True).then_inc(turned, 1)
            pe.wait_ge(have_abs, 1)
            for c in range(KC):
                last = pe.matmul(k.ps[0:P, 2, 0:FEAT], k.ones[:, :], prod[:, c, :], start=(c == 0), stop=(c == KC - 1))
            last.then_inc(bound, 1)


def build(k):
    nc, d = k.nc, k.d
    x_loaded, h_stored = k.sems("build_x"), k.sems("build_h")
    staged, hot, used = k.sem("build_staged"), k.sem("build_hot"), k.sem("build_used")
    staged2, hot2, used2 = k.sem("build_staged2"), k.sem("build_hot2"), k.sem("build_used2")
    evicted, ct_evicted, put, ored = (k.sem("build_" + n) for n in ("evicted", "ct_evicted", "put", "ored"))
    var_ready, rstd_ready, nmr_ready = k.sem("build_var"), k.sem("build_rstd"), k.sem("build_nmr")
    h_ready, hi_ready, lo_ready = k.sem("build_h"), k.sem("build_hi"), k.sem("build_lo")
    c_dve = k.sem("build_c_dve")

    def load(eng, column, n, most=CHUNKS * WINDOWS):
        return eng.value_load(k.table[0:1, bass.ds(n + 128 * column, 1)], min_val=0, max_val=most)

    def further(eng, n, body):
        count, before = load(eng, 1, n, CHUNKS), load(eng, 2, n)
        with eng.If(count > 0):
            with eng.Fori(0, count) as o:
                for part in range(2):
                    body(o, before, part)
        with eng.Else():
            pass

    with nc.Block() as block:

        @block.sync
        def _(sp):
            def load_x(i, par, half):
                wait_past(sp, h_ready, i - 1)
                settle(sp, k)
                sp.dma_start(k.xin[par][:, :], rows(d["x"], i)).then_inc(x_loaded[par], 16)

            def store_h(i, par, half):
                sp.wait_ge(h_ready, i + 1)
                settle(sp, k)
                sp.dma_start(rows(d["h0"], i), k.ho[par][:, :]).then_inc(h_stored[par], 16)

            pipelined(sp, [(0, load_x), (1, store_h)])
            finish_stores(sp, h_stored)

        @block.gpsimd
        def _(pool):
            def put_block(b, par, half):
                pool.wait_ge(evicted, WPT * (b + 1) + 2)
                nc.gpsimd.tensor_copy(k.adj[:, :, :].bitcast(U32)[:, :, bass.ds(b * WORDS, WORDS)],
                                      k.blk[par][:, :].bitcast(U32).rearrange("p (j w) -> p j w", w=WORDS)).then_inc(put, 1)

            def root(i, par, half):
                inverse_deviation(k, pool, i, k.st[par], var_ready, rstd_ready, nmr_ready)

            pipelined(pool, [(0, root), (1, put_block)])

        @block.vector
        def _(dve):
            v = nc.vector
            own = Chain(dve, c_dve, 2)
            dve.sem_inc(hot, 2)
            dve.sem_inc(hot2, 2)

            def one_hots(slot):
                for u in range(QUAD):
                    v.tensor_scalar(k.hot_keys[slot][:, u, 0:KEYS + 1], k.iota_keys[:, 0:KEYS + 1],
                                    k.quad_hi[slot][:, u:u + 1], None, ALU.is_equal)
                low = k.quad_low[slot]
                v.tensor_tensor(k.hot_lo[slot][:, :, 0:P], k.iota_keys[:, 0:P].unsqueeze(1).to_broadcast([P, QUAD, P]),
                                low[:, :, 0:1].to_broadcast([P, QUAD, P]), ALU.is_equal)
                return v.tensor_tensor(k.hot_rel[slot][:, :, :, 0:WIN],
                                       k.iota_keys[:, 0:WIN].unsqueeze(1).unsqueeze(1).to_broadcast([P, QUAD, 2, WIN]),
                                       low[:, :, 1:3].unsqueeze(3).to_broadcast([P, QUAD, 2, WIN]), ALU.is_equal)

            def windows(b, par, half):
                for q in range(WPT):
                    n = WPT * b + q
                    dve.wait_ge(staged, n + 1)
                    dve.wait_ge(used, n + 1)
                    one_hots((par + q) % 2).then_inc(hot, 1)

                    def more(o, before, part):
                        t = 2 * (before + o) + part
                        dve.wait_ge(staged2, t + 1)
                        dve.wait_ge(used2, t + 1)
                        one_hots(2 + part).then_inc(hot2, 1)

                    further(dve, n, more)

            def or_block(b, par, half):
                dve.wait_ge(evicted, WPT * (b + 1) + 2)
                if not isinstance(b, int) or b > 0:
                    dve.wait_ge(ored, b)
                v.tensor_tensor(k.over, k.over, k.blk[par][:, :].bitcast(U32), ALU.bitwise_or).then_inc(ored, 1)

            def stats(i, par, half):
                own.tile(i)
                dve.wait_ge(x_loaded[par], 16 * (half + 1))
                wait_past(dve, h_ready, i - 1)
                statistics(k, dve, own, k.st[par], k.xin[par][:, :], var_ready)

            def low(i, par, half):
                dve.wait_ge(hi_ready, i + 1)
                v.scalar_tensor_tensor(out=k.pairA[:, bass.ds(i, 1), FEAT:2 * FEAT], in0=k.ho[par][:, :].unsqueeze(1), scalar=UP,
                                       in1=k.pairA[:, bass.ds(i, 1), 0:FEAT], op0=ALU.mult,
                                       op1=ALU.subtract).then_inc(lo_ready, 1)

            pipelined(dve, [(0, windows), (1, or_block), (0, stats), (2, low)])

        @block.scalar
        def _(act):
            s = nc.scalar
            act.sem_inc(evicted, 2)
            act.sem_inc(ct_evicted, 2)

            def stage(slot, c, n):
                quad = k.keys[:, bass.ds(c, QUAD), :]
                s.copy(k.quad_hi[slot].unsqueeze(2), quad[:, :, 2:3])
                s.copy(k.quad_low[slot][:, :, 2:3], quad[:, :, 3:4])
                return s.activation(k.quad_low[slot][:, :, 0:2], quad[:, :, 0:2], ACT.Identity,
                                    bias=k.win_off[:, bass.ds(n, 1)])

            def evict(b, par, q):
                n = WPT * b + q
                octets = load(act, 2, n + 1)
                if q == 0:
                    wait_past(act, put, b - 1)
                    wait_past(act, ored, b - 1)
                act.wait_ge(used, n + 1 + 2)
                act.wait_ge(used2, 2 * octets + 2)
                settle(act, k)
                bank = 2 * ((par + q) % 2)
                out = k.blk[par][:, :].rearrange("p (j c) -> p j c", c=PITCH)[:, :, WIN * q:WIN * (q + 1)]
                for a, (j0, j1) in enumerate(((0, HALF_A), (HALF_A, TILES))):
                    last = s.activation(out[:, j0:j1, :], k.ps[0:P, bank + a, 0:(j1 - j0) * WIN]
                                        .rearrange("p (j n) -> p j n", n=WIN), ACT.Copy, scale=1.0 / CNT,
                                        saturate=False)
                last.then_inc(evicted, 1)
                if q == WPT - 1:
                    s.copy(k.CT[:, bass.ds(b, 1), :], k.ps[0:RELS, 4 + par, 0:P].unsqueeze(1)).then_inc(ct_evicted, 1)

            def windows(b, par, half):
                for q in range(WPT):
                    n = WPT * b + q
                    c = load(act, 0, n, CHUNKS - 1)
                    act.wait_ge(hot, n + 1)
                    settle(act, k)
                    stage((par + q) % 2, c, n).then_inc(staged, 1)
                    if q >= 2:
                        evict(b, par, q - 2)
                    elif not isinstance(b, int) or b > 0:
                        evict(b - 1, 1 - par, q - 2 + WPT)

                    def more(o, before, part):
                        t = 2 * (before + o) + part
                        act.wait_ge(hot2, t + 1)
                        settle(act, k)
                        at = nc.s_assert_within(c + 2 * QUAD * o + QUAD * (1 + part), 0, PADDED - QUAD,
                                                skip_runtime_bounds_check_because="the table ends by last chunk + 8")
                        stage(2 + part, at, n).then_inc(staged2, 1)

                    further(act, n, more)

            def h(i, par, half):
                act.wait_ge(nmr_ready, i + 1)
                wait_slot(act, h_stored, par, half)
                wait_past(act, lo_ready, i - 1)
                s.activation(k.ho[par][:, :], k.xin[par][:, :], ACT.Relu, bias=k.st[par][:, 10:11],
                             scale=k.st[par][:, 9:10]).then_inc(h_ready, 1)
                act.wait_ge(h_ready, i + 1)
                s.activation(k.pairA[:, bass.ds(i, 1), 0:FEAT], k.ho[par][:, :].unsqueeze(1), ACT.Copy, scale=UP).then_inc(hi_ready, 1)

            pipelined(act, [(0, windows), (1, h)])
            for q in (WPT - 2, WPT - 1):
                evict(TILES - 1, (TILES - 1) % 2, q)

        @block.tensor
        def _(pe):
            pe.sem_inc(used, 2)
            pe.sem_inc(used2, 2)

            def products(slot, bank, par, q, begin):
                for u in range(QUAD):
                    start = begin and u == 0
                    for a, (j0, j1) in enumerate(((0, HALF_A), (HALF_A, TILES))):
                        pe.matmul(k.ps[0:P, bank + a, 0:(j1 - j0) * WIN], k.hot_lo[slot][:, u, 0:P],
                                  k.hot_keys[slot][:, u, j0 * WIN:j1 * WIN], start=start, stop=True, skip_group_check=True)
                    last = pe.matmul(k.ps[0:RELS, 4 + par, WIN * q:WIN * (q + 1)], k.hot_rel[slot][:, u, 0, 0:RELS],
                                     k.hot_rel[slot][:, u, 1, 0:WIN], start=start, stop=True, skip_group_check=True)
                return last

            def windows(b, par, half):
                pe.wait_ge(ct_evicted, b + 1)
                for q in range(WPT):
                    n = WPT * b + q
                    pe.wait_ge(evicted, n + 1)
                    pe.wait_ge(hot, n + 1 + 2)
                    products((par + q) % 2, 2 * ((par + q) % 2), par, q, True).then_inc(used, 1)

                    def more(o, before, part):
                        pe.wait_ge(hot2, 2 * (before + o) + part + 1 + 2)
                        products(2 + part, 2 * ((par + q) % 2), par, q, False).then_inc(used2, 1)

                    further(pe, n, more)

            pipelined(pe, [(0, windows)])


def degrees(k):
    nc = k.nc
    summed, have_b, have_viol, voted, root = (k.sem("deg_" + n) for n in ("summed", "have_b", "have_viol", "voted", "root"))
    ok, cleared = k.sem("deg_ok"), k.sem("deg_cleared")
    with nc.Block() as block:

        @block.tensor
        def _(pe):
            for i in range(TILES):
                last = pe.matmul(k.ps[0:P, 0, i:i + 1], k.CT[:, i, :], k.ones[0:RELS, 0:1], start=True, stop=True)
            last.then_inc(summed, 1)
            pe.wait_ge(have_viol, 1)
            pe.matmul(k.ps[0:1, 1, 0:2], k.ones[0:P, 0:1], k.st[0][:, 0:2], start=True, stop=True).then_inc(voted, 1)

        @block.gpsimd
        def _(pool):
            pool.wait_ge(have_b, 1)
            nc.gpsimd.tensor_tensor(k.dinv[:, 0:TILES], k.dinv[:, 0:TILES], k.mhalf[:, 0:TILES], ALU.pow).then_inc(root, 1)

        @block.vector
        def _(dve):
            v = nc.vector
            own = Chain(dve, ok, 100).tile(0)
            n = slice(0, TILES)
            dve.wait_ge(summed, 1)
            own.link(v.tensor_copy(k.indeg[:, n], k.ps[0:P, 0, n]))
            own.link(v.tensor_scalar(k.dinv[:, n], k.indeg[:, n], 1.0, None, ALU.add))
            dve.sem_inc(have_b, 1)
            own.link(v.tensor_reduce(k.st[0][:, 1:2], k.indeg[:, n], AX.X, ALU.add))
            own.link(v.tensor_scalar(k.over, k.over, 0x40404040, None, ALU.bitwise_and))
            own.link(v.tensor_reduce(k.st[0][:, 0:1], k.over, AX.X, ALU.max))
            dve.sem_inc(have_viol, 1)
            own.link(v.tensor_scalar(k.rsB[:, n], k.indeg[:, n], 1.0, None, ALU.max))
            own.link(v.reciprocal(k.rsB[:, n], k.rsB[:, n]))
            own.link(v.tensor_scalar(k.rsD[:, n], k.indeg[:, n], 0.0, CNT, ALU.is_gt, ALU.mult))
            own.link(v.tensor_tensor(k.rsB[:, n], k.rsB[:, n], k.rsD[:, n], ALU.mult))
            dve.wait_ge(root, 1)
            own.link(v.tensor_scalar(k.dinvs[:, n], k.dinv[:, n], CNT / UP, None, ALU.mult))
            own.link(v.tensor_scalar(k.dinvu[:, n], k.dinv[:, n], UP, None, ALU.mult))
            dve.wait_ge(voted, 1)
            own.link(v.tensor_scalar(k.st[1][0:1, 0:1], k.ps[0:1, 1, 1:2], float(EDGES), None, ALU.not_equal))
            own.link(v.tensor_scalar(k.st[1][0:1, 1:2], k.ps[0:1, 1, 0:1], 0.0, None, ALU.is_gt))
            own.link(v.tensor_tensor(k.flag[:, :], k.st[1][0:1, 0:1], k.st[1][0:1, 1:2], ALU.max))

            def run(general):
                if general:
                    v.memset(k.adj[:, :, :].bitcast(U32), 0).then_inc(cleared, 1)
                    dve.wait_ge(cleared, 1)

            either(dve, k, run)


def split_scaled(k, s, dst, i, t, scale):
    return s.activation(dst[:, bass.ds(i, 1), 0:FEAT], t[:, :].unsqueeze(1), ACT.Copy, scale=scale)


def mean_by_destination(k, name, src, dst, store, second):
    nc = k.nc
    acc_ready, acc_free, copied = (k.sem(f"{name}_{n}") for n in ("acc", "acc_free", "copied"))
    aw_ready, t_ready, hi_ready, lo_ready = (k.sem(f"{name}_{n}") for n in ("aw", "t", "hi", "lo"))
    stored = k.sems(name + "_stored")
    whh_loaded = k.sem(name + "_whh") if second else None
    extra_ready = k.sems(name + "_extra")
    with nc.Block() as block:

        @block.sync
        def _(sp):
            def put(i, par, half):
                sp.wait_ge(t_ready, i + 1)
                settle(sp, k)
                sp.dma_start(rows(store, i), k.t[par][:, :]).then_inc(stored[par], 16)

            if second:
                sp.dma_start(k.whh[:, :, :], k.d["w_hhT"].rearrange("(c f) n -> f c n", f=128)).then_inc(whh_loaded, 16)
            either(sp, k, lambda general: pipelined(sp, (
                [(0, extra_loads(k, sp, acc_ready, extra_ready))] if general else []) + [(0, put)]))
            finish_stores(sp, stored)
            if second:
                sp.wait_ge(whh_loaded, 16)

        @block.gpsimd
        def _(pool):
            stage_columns(k, pool, copied, acc_ready)

        @block.tensor
        def _(pe):
            def run(general):
                def agg(i, par, half):
                    pe.wait_ge(copied, i + 1)
                    wait_past(pe, t_ready, i - 1)
                    aggregate(k, pe, par, half, src, extra_ready if general else None).then_inc(acc_ready, 1)

                pipelined(pe, [(0, agg)])

            either(pe, k, run)

        @block.scalar
        def _(act):
            def scale_high(i, par, half):
                act.wait_ge(acc_ready, i + 1)
                wait_past(act, t_ready, i - 1)
                nc.scalar.activation(k.aw[par][:, :], k.ps[0:P, par, 0:FEAT], ACT.Copy,
                                     scale=k.rsB[:, bass.ds(i, 1)]).then_inc(aw_ready, 1)
                act.wait_ge(t_ready, i + 1)
                split_scaled(k, nc.scalar, dst, i, k.t[par], 1.0).then_inc(hi_ready, 1)

            pipelined(act, [(0, scale_high)])

        @block.vector
        def _(dve):
            v = nc.vector

            def combine(i, par, half):
                dve.wait_ge(aw_ready, i + 1)
                if not isinstance(half, int) or half > 0:
                    dve.wait_ge(stored[par], 16 * half)
                v.scalar_tensor_tensor(out=k.t[par][:, :], in0=k.ps[0:P, par, FEAT:2 * FEAT],
                                       scalar=k.rsB[:, bass.ds(i, 1)], in1=k.aw[par][:, :],
                                       op0=ALU.mult, op1=ALU.add).then_inc(t_ready, 1)
                dve.wait_ge(hi_ready, i + 1)
                v.tensor_tensor(dst[:, bass.ds(i, 1), FEAT:2 * FEAT], k.t[par][:, :].unsqueeze(1),
                                dst[:, bass.ds(i, 1), 0:FEAT], ALU.subtract).then_inc(lo_ready, 1)

            pipelined(dve, [(0, combine)])


def stage_columns(k, pool, copied, used):
    def copy(i, par, half):
        wait_past(pool, used, i - 1)
        copy_columns(k, i, par).then_inc(copied, 1)

    pipelined(pool, [(0, copy)])


def aggregate(k, pe, par, half, src, extra_ready=None):
    settle(pe, k)
    a = k.blk[par][:, :].rearrange("p (j c) -> p j c", c=PITCH)
    for j in range(TILES):
        if j == TILES - 1 and extra_ready is not None:
            pe.wait_ge(extra_ready[par], 16 * (half + 1))
            pe.matmul(k.ps[0:P, par, 0:FEAT], k.ident[:, 0:P], k.extra[par][:, :], start=False, stop=False)
        last = pe.matmul(k.ps[0:P, par, :], a[:, j, 0:P], src[:, j, :], start=(j == 0), stop=(j == TILES - 1))
    return last


def extra_loads(k, sp, acc, extra_ready):
    def load_extra(i, par, half):
        wait_past(sp, acc, i - 1)
        settle(sp, k)
        sp.dma_start(k.extra[par][:, :], rows(k.d["extra"], i)).then_inc(extra_ready[par], 16)

    return load_extra


def finish_stores(eng, stored):
    for par in range(2):
        eng.wait_ge(stored[par], 16 * ((TILES + 1 - par) // 2))


def wait_slot(eng, sems, par, half):
    if not isinstance(half, int) or half > 0:
        eng.wait_ge(sems[par], 16 * half)


def turn(k, pe, bank, at, tile):
    for c in range(KC):
        last = pe.transpose(k.ps[0:128, bank, at + c * P:at + (c + 1) * P], tile[:, 128 * c:128 * (c + 1)], k.ident[:, 0:P])
    return last


def product(k, pe, out, tT, w):
    for c in range(KC):
        last = pe.matmul(out, tT[:, c, :], w[:, c, :], start=(c == 0), stop=(c == KC - 1))
    return last


def scatter_mean(k, name, src, first):
    nc, d = k.nc, k.d
    S = {n: k.sem(f"{name}_{n}") for n in (
        "row", "flipped", "flip_a", "flip_v", "degree", "scale", "blk", "acc", "aw", "t", "turned", "tT", "product",
        "u", "x", "hi", "lo", "var", "rstd", "nmr", "h", "own_a", "own_v", "own_w")}
    kept, loaded_b = k.sems(name + "_kept"), k.sems(name + "_loaded_b")
    loaded_x, stored_x, stored_h = k.sems(name + "_loaded_x"), k.sems(name + "_stored_x"), k.sems(name + "_stored_h")
    W, bias = (k.W1, k.b1) if first else (k.W2, k.b2)
    agg_lag = 1 if first else 0
    rs = k.rsD if first else k.rsD4
    extra_ready = k.sems(name + "_extra")
    GROUPS = [(4 * g, min(4 * g + 4, TILES)) for g in range((TILES + 3) // 4)]

    with nc.Block() as block:

        @block.sync
        def _(sp):
            def keep_block(i, par, half):
                sp.wait_ge(S["flip_a"], 4 * (i + 1))
                settle(sp, k)
                sp.wait_ge(S["flip_v"], 3 * (i + 1))
                settle(sp, k)
                sp.dma_start(d["adjT"][bass.ds(i, 1), :, :].rearrange("o p w -> p (o w)"),
                             k.blk[par][:, :].bitcast(U32)).then_inc(kept[par], 16)

            def load_block(i, par, half):
                wait_past(sp, S["acc"], i - 1)
                settle(sp, k)
                sp.dma_start(k.blk[par][:, :].bitcast(U32),
                             d["adjT"][bass.ds(i, 1), :, :].rearrange("o p w -> p (o w)")).then_inc(loaded_b[par], 16)

            def load_xh(i, par, half):
                wait_past(sp, S["x"], i - 1)
                settle(sp, k)
                sp.dma_start(k.xin[par][:, :], rows(d["x"], i)).then_inc(loaded_x[par], 16)
                sp.dma_start(k.hin[par][:, :], rows(d["h0"], i)).then_inc(loaded_x[par], 16)

            def store_g(i, par, half):
                sp.wait_ge(S["x"], i + 1)
                settle(sp, k)
                sp.dma_start(rows(d["g"], i), k.xo[par][:, :]).then_inc(stored_x[par], 16)

            def store_x(i, par, half):
                sp.wait_ge(S["x"], i + 1)
                settle(sp, k)
                sp.dma_start(rows(d["x1"], i), k.xo[par][:, :]).then_inc(stored_x[par], 16)
                sp.wait_ge(S["h"], i + 1)
                settle(sp, k)
                sp.dma_start(rows(d["h1"], i), k.ho[par][:, :]).then_inc(stored_h[par], 16)

            stages = [(0, keep_block), (4, store_g)] if first else [(0, load_block), (1, load_xh), (4, store_x)]
            either(sp, k, lambda general: pipelined(sp, (
                [(agg_lag, extra_loads(k, sp, S["acc"], extra_ready))] if general else []) + stages))
            finish_stores(sp, kept if first else stored_h)
            finish_stores(sp, stored_x)

        @block.gpsimd
        def _(pool):
            def copy_row(i, par, half):
                wait_past(pool, S["flipped"], len(GROUPS) * (i - 1))
                wait_past(pool, S["degree"], i - 1)
                nc.gpsimd.tensor_copy(k.row[par][:, :].bitcast(U32),
                                      k.adj[:, bass.ds(i, 1), :].bitcast(U32).rearrange("p o w -> p (o w)")
                                      ).then_inc(S["row"], 1)

            def root(i, par, half):
                inverse_deviation(k, pool, i, k.st[par], S["var"], S["rstd"], S["nmr"])

            pipelined(pool, [(0, copy_row)] if first else [(3, root)])

        @block.tensor
        def _(pe):
            def run(general):
                def flip(i, par, half):
                    pe.wait_ge(S["row"], i + 1)
                    row = k.row[par][:, :].rearrange("p (j c) -> p j c", c=PITCH)
                    for g, (j0, j1) in enumerate(GROUPS):
                        sem, n = (("flip_a", 4 * i + (-1, 0, 1, 2)[g // 2]) if g % 2 == 0 else
                                  ("flip_v", 3 * i + (0, -1, 1)[g // 2]))
                        wait_past(pe, S[sem], n)
                        settle(pe, k)
                        for j in range(j0, j1):
                            last = pe.matmul(k.ps[0:P, 4 + g % 4, (j - j0) * P:(j - j0 + 1) * P], row[:, j, 0:P],
                                             k.identb[:, 0:P], start=True, stop=True)
                        last.then_inc(S["flipped"], 1)

                def agg(i, par, half):
                    if first:
                        pe.wait_ge(S["flip_a"], 4 * (i + 1))
                        pe.wait_ge(S["flip_v"], 3 * (i + 1))
                    else:
                        pe.wait_ge(loaded_b[par], 16 * (half + 1))
                    wait_past(pe, S["t"], i - 1)
                    aggregate(k, pe, par, half, src, extra_ready if general else None).then_inc(S["acc"], 1)

                def turn_t(i, par, half):
                    pe.wait_ge(S["t"], i + 1)
                    wait_past(pe, S["tT"], i)
                    turn(k, pe, 2, 0, k.t[par]).then_inc(S["turned"], 1)

                def dense(i, par, half):
                    pe.wait_ge(S["tT"], i + 1)
                    wait_past(pe, S["u"], i)
                    product(k, pe, k.ps[0:P, 3, 0:FEAT], k.tT[par], W).then_inc(S["product"], 1)

                pipelined(pe, ([(0, flip)] if first else []) + [(agg_lag, agg), (agg_lag + 1, turn_t), (agg_lag + 2, dense)])

            either(pe, k, run)

        @block.scalar
        def _(act):
            s = nc.scalar

            def flip_out(i, par, half):
                wait_past(act, S["acc"], i - 1)
                wait_slot(act, kept, par, half)
                blk = k.blk[par][:, :].rearrange("p (j c) -> p j c", c=PITCH)
                for g in (0, 2, 4, 6):
                    j0, j1 = GROUPS[g]
                    act.wait_ge(S["flipped"], len(GROUPS) * i + g + 1)
                    settle(act, k)
                    s.activation(blk[:, j0:j1, 0:P], k.ps[0:P, 4 + g % 4, 0:(j1 - j0) * P].rearrange("p (j c) -> p j c", c=P),
                                 ACT.Copy, saturate=False).then_inc(S["flip_a"], 1)

            own_a = Chain(act, S["own_a"], 1)

            def degree(i, par, half):
                act.wait_ge(S["row"], i + 1)
                wait_past(act, S["scale"], i - 1)
                settle(act, k)
                s.activation(k.junk[:, :], k.row[par][:, :], ACT.Copy, saturate=False,
                             accum_out=k.st[par][:, 14:15]).then_inc(S["degree"], 1)

            def scale_high(i, par, half):
                act.wait_ge(S["acc"], i + 1)
                if first:
                    act.wait_ge(S["scale"], i + 1)
                wait_past(act, S["t"], i - 1)
                s.activation(k.aw[par][:, :], k.ps[0:P, par, 0:FEAT], ACT.Copy,
                             scale=rs[:, bass.ds(i, 1)]).then_inc(S["aw"], 1)

            def tT_out(i, par, half):
                act.wait_ge(S["turned"], i + 1)
                wait_past(act, S["product"], i - 1)
                s.copy(k.tT[par][:, 0:KC, :], k.ps[0:128, 2, 0:2 * P]
                       .rearrange("f (c p) -> f c p", p=P)).then_inc(S["tT"], 1)

            def split(i, par, half):
                if first:
                    act.wait_ge(S["x"], i + 1)
                    split_scaled(k, s, k.pairA, i, k.xo[par], 1.0).then_inc(S["hi"], 1)
                else:
                    wait_slot(act, stored_h, par, half)
                    wait_past(act, S["lo"], i - 1)
                    act.wait_ge(S["nmr"], i + 1)
                    s.activation(k.ho[par][:, :], k.xo[par][:, :], ACT.Relu, bias=k.st[par][:, 10:11],
                                 scale=k.st[par][:, 9:10]).then_inc(S["h"], 1)
                    act.wait_ge(S["h"], i + 1)
                    split_scaled(k, s, k.pairA, i, k.ho[par], UP).then_inc(S["hi"], 1)

            pipelined(act, ([(0, flip_out), (0, degree)] if first else []) +
                      [(4, split), (agg_lag, scale_high), (agg_lag + 1, tT_out)])

        @block.vector
        def _(dve):
            v = nc.vector
            stt = v.scalar_tensor_tensor
            own_v = Chain(dve, S["own_v"], 4)
            own_w = Chain(dve, S["own_w"], 2 if first else 5)

            def flip_out(i, par, half):
                wait_past(dve, S["acc"], i - 1)
                wait_slot(dve, kept, par, half)
                blk = k.blk[par][:, :].rearrange("p (j c) -> p j c", c=PITCH)
                for g in (1, 3, 5):
                    j0, j1 = GROUPS[g]
                    dve.wait_ge(S["flipped"], len(GROUPS) * i + g + 1)
                    settle(dve, k)
                    v.tensor_copy(blk[:, j0:j1, 0:P], k.ps[0:P, 4 + g % 4, 0:(j1 - j0) * P]
                                  .rearrange("p (j c) -> p j c", c=P), saturate=False).then_inc(S["flip_v"], 1)

            def scale(i, par, half):
                own_v.tile(i)
                dve.wait_ge(S["degree"], i + 1)
                q, r = k.st[par][:, 15:16], k.st[par][:, 12:13]
                own_v.link(v.tensor_tensor(q, k.st[par][:, 14:15], k.odeg8[:, bass.ds(i, 1)], ALU.add))
                own_v.link(v.tensor_scalar(r, q, 1.0 / CNT, UP, ALU.max, ALU.mult))
                own_v.link(v.reciprocal(r, r))
                own_v.link(v.tensor_scalar(k.st[par][:, 13:14], q, 0.0, None, ALU.is_gt))
                v.tensor_tensor(k.rsD[:, bass.ds(i, 1)], r, k.st[par][:, 13:14], ALU.mult).then_inc(S["scale"], 1)

            def combine(i, par, half):
                dve.wait_ge(S["aw"], i + 1)
                wait_past(dve, S["turned"], i - 1)
                stt(out=k.t[par][:, :], in0=k.ps[0:P, par, FEAT:2 * FEAT], scalar=rs[:, bass.ds(i, 1)],
                    in1=k.aw[par][:, :], op0=ALU.mult, op1=ALU.add).then_inc(S["t"], 1)

            def after_g(i, par, half):
                own_w.tile(i)
                ps = k.ps[0:P, 3, 0:FEAT]
                u, p, g = k.hin[par], k.ho[par], k.xo[par]
                dve.wait_ge(S["product"], i + 1)
                wait_past(dve, S["x"], i - 1)
                v.tensor_tensor(u[:, :], ps, bias[:, :], ALU.add).then_inc(S["u"], 1)
                dve.wait_ge(S["u"], i + 1)
                own_w.link(v.tensor_scalar(p[:, :], u[:, :], 0.0, k.gscale[:, :], ALU.max, ALU.mult))
                own_w.link(v.tensor_scalar(u[:, :], u[:, :], 0.0, k.gslope[:, :], ALU.min, ALU.mult))
                wait_slot(dve, stored_x, par, half)
                wait_past(dve, S["lo"], i - 1)
                v.tensor_tensor(g[:, :], u[:, :], p[:, :], ALU.add).then_inc(S["x"], 1)

            def low_g(i, par, half):
                g = k.xo[par]
                dve.wait_ge(S["hi"], i + 1)
                v.tensor_tensor(k.pairA[:, bass.ds(i, 1), FEAT:2 * FEAT], g[:, :].unsqueeze(1),
                                k.pairA[:, bass.ds(i, 1), 0:FEAT], ALU.subtract).then_inc(S["lo"], 1)

            def after_x(i, par, half):
                own_w.tile(i)
                ps = k.ps[0:P, 3, 0:FEAT]
                u, x, st = k.hin[par], k.xo[par], k.st[par]
                dve.wait_ge(loaded_x[par], 32 * (half + 1))
                own_w.link(v.tensor_tensor(u[:, :], u[:, :], bias[:, :], ALU.add))
                dve.wait_ge(S["product"], i + 1)
                v.tensor_tensor(u[:, :], ps, u[:, :], ALU.add).then_inc(S["u"], 1)
                dve.wait_ge(S["u"], i + 1)
                wait_slot(dve, stored_x, par, half)
                wait_past(dve, S["h"], i - 1)
                own_w.link(v.tensor_scalar(x[:, :], u[:, :], 0.0, k.slope[:, :], ALU.min, ALU.mult))
                own_w.link(stt(out=x[:, :], in0=u[:, :], scalar=0.0, in1=x[:, :], op0=ALU.max, op1=ALU.add))
                v.tensor_tensor(x[:, :], x[:, :], k.xin[par][:, :], ALU.add).then_inc(S["x"], 1)
                dve.wait_ge(S["x"], i + 1)
                statistics(k, dve, own_w, st, x[:, :], S["var"])

            def low_h(i, par, half):
                dve.wait_ge(S["hi"], i + 1)
                stt(out=k.pairA[:, bass.ds(i, 1), FEAT:2 * FEAT], in0=k.ho[par][:, :].unsqueeze(1), scalar=UP,
                    in1=k.pairA[:, bass.ds(i, 1), 0:FEAT], op0=ALU.mult, op1=ALU.subtract).then_inc(S["lo"], 1)

            pipelined(dve, ([(0, flip_out), (0, scale)] if first else []) +
                      [(5, low_g if first else low_h), (agg_lag + 3, after_g if first else after_x),
                       (agg_lag, combine)])
            if first:
                dve.wait_ge(S["scale"], TILES)
                v.tensor_scalar(k.rsD4[:, 0:TILES], k.rsD[:, 0:TILES], UP / CNT, k.gunscale[:, :],
                                ALU.mult, ALU.mult).then_inc(S["scale"], 1)
                dve.wait_ge(S["scale"], TILES + 1)


def gru(k):
    nc, d = k.nc, k.d
    S = {n: k.sem("gru_" + n) for n in ("copied", "acc", "aw", "t", "turned", "tT", "product", "u", "x", "hi",
                                        "lo", "var", "rstd", "nmr", "h", "rz", "gates", "pre", "new", "own", "own2")}
    extra_ready = k.sems("gru_extra")
    loaded, loaded_c, stored_x, stored_h = k.sems("gru_loaded"), k.sems("gru_loaded_c"), k.sems("gru_stored_x"), k.sems("gru_stored_h")
    units = [r[:, :].bitcast(F32)[:, FEAT * n:FEAT * (n + 1)] for r in k.row for n in range(3)]
    rz = [k.W1[0:P, :, :].rearrange("p c n -> p (c n)"), k.row[0][:, :].bitcast(F32)[:, 0:2 * FEAT]]
    tmp, new = (units[2], units[3]), (units[4], units[5])
    hold = [k.W2[0:P, n, :] for n in range(2)]
    with nc.Block() as block:

        @block.sync
        def _(sp):
            def load(i, par, half):
                wait_past(sp, S["turned"], i - 1)
                settle(sp, k)
                sp.dma_start(k.hin[par][:, :], rows(d["h1"], i)).then_inc(loaded[par], 16)

            def load_cell(i, par, half):
                wait_past(sp, S["x"], i - 1)
                settle(sp, k)
                sp.dma_start(k.xin[par][:, :], rows(d["x1"], i)).then_inc(loaded_c[par], 16)
                sp.dma_start(hold[par], rows(d["h1"], i)).then_inc(loaded_c[par], 16)

            def store(i, par, half):
                sp.wait_ge(S["x"], i + 1)
                settle(sp, k)
                sp.dma_start(rows(d["x2"], i), k.xo[par][:, :]).then_inc(stored_x[par], 16)
                sp.wait_ge(S["h"], i + 1)
                settle(sp, k)
                sp.dma_start(rows(d["s2"], i), k.ho[par][:, :]).then_inc(stored_h[par], 16)

            either(sp, k, lambda general: pipelined(sp, (
                [(0, extra_loads(k, sp, S["acc"], extra_ready))] if general else []) + [(0, load), (3, load_cell), (6, store)]))
            finish_stores(sp, stored_x)
            finish_stores(sp, stored_h)

        @block.gpsimd
        def _(pool):
            def copy(i, par, half):
                wait_past(pool, S["acc"], i - 1)
                copy_columns(k, i, par).then_inc(S["copied"], 1)

            def root(i, par, half):
                inverse_deviation(k, pool, i, k.st[par], S["var"], S["rstd"], S["nmr"], k.dinvu)

            pipelined(pool, [(0, copy), (5, root)])

        @block.tensor
        def _(pe):
            def run(general):
                def agg(i, par, half):
                    pe.wait_ge(S["copied"], i + 1)
                    wait_past(pe, S["t"], i - 1)
                    aggregate(k, pe, par, half, k.pairA, extra_ready if general else None).then_inc(S["acc"], 1)

                def turn_both(i, par, half):
                    pe.wait_ge(S["t"], i + 1)
                    pe.wait_ge(loaded[par], 16 * (half + 1))
                    wait_past(pe, S["tT"], i - 1)
                    for c in range(KC):
                        out = k.ps[0:128, 2 + par, c * P:(c + 1) * P]
                        pe.matmul(out, k.rel[:, 128 * c:128 * (c + 1)],
                                  k.CT[:, bass.ds(i, 1), :].rearrange("r o p -> r (o p)"), start=True, stop=False)
                        pe.matmul(out, k.t[par][:, 128 * c:128 * (c + 1)], k.ident[:, 0:P], start=False, stop=True)
                    turn(k, pe, 2 + par, 2 * P, k.hin[par]).then_inc(S["turned"], 1)

                def dense(i, par, half):
                    pe.wait_ge(S["tT"], i + 1)
                    wait_past(pe, S["u"], i - 1)
                    red, h = k.tT[par][:, 0:KC, :], k.tT[par][:, KC:2 * KC, :]
                    rz, new = k.ps[0:P, 4 + 2 * par, :], k.ps[0:P, 5 + 2 * par, :]
                    for n, (x, w) in enumerate(((red, k.wih), (h, k.whh))):
                        for c in range(KC):
                            pe.matmul(rz, x[:, c, :], w[:, c, 0:2 * FEAT], start=(n + c == 0), stop=(n + c == 2))
                    product(k, pe, new[:, 0:FEAT], red, k.wih[:, :, 2 * FEAT:3 * FEAT])
                    product(k, pe, new[:, FEAT:2 * FEAT], h, k.whh[:, :, 2 * FEAT:3 * FEAT]).then_inc(S["product"], 1)

                pipelined(pe, [(0, agg), (1, turn_both), (2, dense)])

            either(pe, k, run)

        @block.scalar
        def _(act):
            s = nc.scalar

            def scale_high(i, par, half):
                act.wait_ge(S["acc"], i + 1)
                wait_past(act, S["t"], i - 1)
                s.activation(k.aw[par][:, :], k.ps[0:P, par, 0:FEAT], ACT.Copy, scale=CNT / UP).then_inc(S["aw"], 1)

            def tT_out(i, par, half):
                act.wait_ge(S["turned"], i + 1)
                wait_past(act, S["product"], i - 1)
                s.copy(k.tT[par][:, :, :], k.ps[0:128, 2 + par, 0:2 * KC * P]
                       .rearrange("f (c p) -> f c p", p=P)).then_inc(S["tT"], 1)

            def gates(i, par, half):
                act.wait_ge(S["rz"], i + 1)
                s.activation(rz[par], rz[par], ACT.Sigmoid).then_inc(S["gates"], 1)

            def squash(i, par, half):
                act.wait_ge(S["pre"], i + 1)
                s.activation(new[par], new[par], ACT.Tanh).then_inc(S["new"], 1)

            def split(i, par, half):
                act.wait_ge(S["nmr"], i + 1)
                wait_past(act, S["lo"], i - 1)
                wait_slot(act, stored_h, par, half)
                s.activation(k.ho[par][:, :], k.xo[par][:, :], ACT.Relu, bias=k.st[par][:, 10:11],
                             scale=k.st[par][:, 9:10]).then_inc(S["h"], 1)
                act.wait_ge(S["h"], i + 1)
                split_scaled(k, s, k.pairB, i, k.ho[par], 1.0).then_inc(S["hi"], 1)

            pipelined(act, [(6, split), (4, squash), (3, gates), (0, scale_high), (1, tT_out)])

        @block.vector
        def _(dve):
            v = nc.vector
            stt = v.scalar_tensor_tensor
            own, own2 = Chain(dve, S["own"], 1), Chain(dve, S["own2"], 5)

            def combine(i, par, half):
                dve.wait_ge(S["aw"], i + 1)
                wait_past(dve, S["turned"], i - 1)
                stt(out=k.t[par][:, :], in0=k.ps[0:P, par, FEAT:2 * FEAT], scalar=CNT / UP, in1=k.aw[par][:, :],
                    op0=ALU.mult, op1=ALU.add).then_inc(S["t"], 1)

            def biases(i, par, half):
                gate, value = k.ps[0:P, 4 + 2 * par, :], k.ps[0:P, 5 + 2 * par, :]
                dve.wait_ge(S["product"], i + 1)
                v.tensor_tensor(rz[par], gate, k.bi[:, 0:2 * FEAT], ALU.add).then_inc(S["rz"], 1)
                v.tensor_tensor(tmp[par], value[:, 0:FEAT], k.bi[:, 2 * FEAT:3 * FEAT], ALU.add)
                v.tensor_tensor(new[par], value[:, FEAT:2 * FEAT], k.bhn[:, :], ALU.add).then_inc(S["u"], 1)

            def reset(i, par, half):
                own.tile(i)
                dve.wait_ge(S["u"], i + 1)
                dve.wait_ge(S["gates"], i + 1)
                own.link(v.tensor_tensor(new[par], new[par], rz[par][:, 0:FEAT], ALU.mult))
                v.tensor_tensor(new[par], new[par], tmp[par], ALU.add).then_inc(S["pre"], 1)

            def cell(i, par, half):
                own2.tile(i)
                x, st = k.xo[par], k.st[par]
                dve.wait_ge(loaded_c[par], 32 * (half + 1))
                dve.wait_ge(S["new"], i + 1)
                own2.link(v.tensor_tensor(tmp[par], hold[par], new[par], ALU.subtract))
                own2.link(v.tensor_tensor(tmp[par], tmp[par], rz[par][:, FEAT:2 * FEAT], ALU.mult))
                own2.link(v.tensor_tensor(tmp[par], tmp[par], new[par], ALU.add))
                wait_slot(dve, stored_x, par, half)
                wait_past(dve, S["h"], i - 1)
                v.tensor_tensor(x[:, :], tmp[par], k.xin[par][:, :], ALU.add).then_inc(S["x"], 1)
                dve.wait_ge(S["x"], i + 1)
                statistics(k, dve, own2, st, x[:, :], S["var"])

            def low(i, par, half):
                dve.wait_ge(S["hi"], i + 1)
                v.tensor_tensor(k.pairB[:, bass.ds(i, 1), FEAT:2 * FEAT], k.ho[par][:, :].unsqueeze(1),
                                k.pairB[:, bass.ds(i, 1), 0:FEAT], ALU.subtract).then_inc(S["lo"], 1)

            pipelined(dve, [(7, low), (5, cell), (4, reset), (3, biases), (0, combine)])


def inverse_deviation(k, pool, i, st, var, rstd, nmr, scale=None):
    pool.wait_ge(var, i + 1)
    k.nc.gpsimd.tensor_tensor(st[:, 9:10], st[:, 8:9], k.mhalf[:, 0:1], ALU.pow).then_inc(rstd, 1)
    per = 1
    if scale is not None:
        per = 2
        pool.wait_ge(rstd, 2 * i + 1)
        settle(pool, k)
        k.nc.gpsimd.tensor_tensor(st[:, 9:10], st[:, 9:10], scale[:, bass.ds(i, 1)], ALU.mult).then_inc(rstd, 1)
    pool.wait_ge(rstd, per * (i + 1))
    k.nc.gpsimd.tensor_tensor(st[:, 10:11], st[:, 7:8], st[:, 9:10], ALU.mult).then_inc(nmr, 1)


def statistics(k, dve, own, st, x, var):
    v = k.nc.vector
    own.link(v.bn_stats(st[:, 0:6], x))
    settle(dve, k)
    own.link(v.bn_aggr(st[:, 11:13], st[:, 0:6]))
    v.tensor_scalar(st[:, 7:8], st[:, 11:12], -1.0, None, ALU.mult)
    v.tensor_scalar(st[:, 8:9], st[:, 12:13], EPS, None, ALU.add).then_inc(var, 1)


def copy_columns(k, i, par):
    return k.nc.gpsimd.tensor_copy(k.blk[par][:, :].bitcast(U32).rearrange("p (j w) -> p j w", w=WORDS),
                                   k.adj[:, :, :].bitcast(U32)[:, :, bass.ds(i * WORDS, WORDS)])


def gcn(k):
    nc, d = k.nc, k.d
    S = {n: k.sem("gcn_" + n) for n in ("copied", "acc", "aw", "t", "turned", "tT", "product", "u", "x", "y", "var", "rstd", "nmr", "h",
                                        "turned2", "tT2", "product2", "var2", "rstd2", "nmr2",
                                        "z", "own", "own2", "own3")}
    c2 = [k.row[0][:, :].bitcast(F32)[:, ZW + FEAT * n:ZW + FEAT * (n + 1)] for n in range(2)]
    extra_ready = k.sems("gcn_extra")
    loaded, loaded_x, stored = k.sems("gcn_loaded"), k.sems("gcn_loaded_x"), k.sems("gcn_stored")
    with nc.Block() as block:

        @block.sync
        def _(sp):
            def load_s(i, par, half):
                wait_past(sp, S["t"], i - 1)
                settle(sp, k)
                sp.dma_start(k.hin[par][:, :], rows(d["s2"], i)).then_inc(loaded[par], 16)

            def load_x(i, par, half):
                wait_past(sp, S["x"], i - 1)
                settle(sp, k)
                sp.dma_start(k.xin[par][:, :], rows(d["x2"], i)).then_inc(loaded_x[par], 16)

            def store(i, par, half):
                sp.wait_ge(S["z"], i + 1)
                settle(sp, k)
                sp.dma_start(rows(d["z"], i), k.z[par][:, :]).then_inc(stored[par], 16)
                sp.dma_start(rows(d["alpha_l"], i), k.z[par][:, FEAT + HEADS:ZW]).then_inc(stored[par], 16)

            either(sp, k, lambda general: pipelined(sp, (
                [(0, extra_loads(k, sp, S["acc"], extra_ready))] if general else []) + [(0, load_s), (4, load_x), (9, store)]))
            for par in range(2):
                sp.wait_ge(stored[par], 32 * ((TILES + 1 - par) // 2))

        @block.gpsimd
        def _(pool):
            def copy(i, par, half):
                wait_past(pool, S["acc"], i - 1)
                copy_columns(k, i, par).then_inc(S["copied"], 1)

            def root_c(i, par, half):
                inverse_deviation(k, pool, i, k.st[par], S["var"], S["rstd"], S["nmr"])

            def root_x(i, par, half):
                inverse_deviation(k, pool, i, k.st2[par], S["var2"], S["rstd2"], S["nmr2"])

            pipelined(pool, [(0, copy), (5, root_x), (3, root_c)])

        @block.tensor
        def _(pe):
            def run(general):
                def agg(i, par, half):
                    pe.wait_ge(S["copied"], i + 1)
                    wait_past(pe, S["t"], i - 1)
                    aggregate(k, pe, par, half, k.pairB, extra_ready if general else None).then_inc(S["acc"], 1)

                def turn_t(i, par, half):
                    pe.wait_ge(S["t"], i + 1)
                    wait_past(pe, S["tT"], i)
                    turn(k, pe, 2, 0, k.t[par]).then_inc(S["turned"], 1)

                def dense(i, par, half):
                    pe.wait_ge(S["tT"], i + 1)
                    wait_past(pe, S["u"], i)
                    product(k, pe, k.ps[0:P, 3, 0:FEAT], k.tT[par], k.Wg).then_inc(S["product"], 1)

                def turn_h(i, par, half):
                    pe.wait_ge(S["h"], i + 1)
                    wait_past(pe, S["tT2"], i)
                    turn(k, pe, 4, 0, k.ho[par]).then_inc(S["turned2"], 1)

                def dense_z(i, par, half):
                    pe.wait_ge(S["tT2"], i + 1)
                    wait_past(pe, S["z"], i - 1)
                    product(k, pe, k.ps[0:P, 5 + par, 0:ZW], k.tT[par][:, KC:2 * KC, :], k.Wz).then_inc(S["product2"], 1)

                pipelined(pe, [(0, agg), (1, turn_t), (2, dense), (7, turn_h), (8, dense_z)])

            either(pe, k, run)

        @block.scalar
        def _(act):
            s = nc.scalar

            def scale_high(i, par, half):
                act.wait_ge(S["acc"], i + 1)
                wait_past(act, S["t"], i - 1)
                s.activation(k.aw[par][:, :], k.ps[0:P, par, 0:FEAT], ACT.Copy,
                             scale=k.dinvs[:, bass.ds(i, 1)]).then_inc(S["aw"], 1)

            def tT_out(i, par, half):
                act.wait_ge(S["turned"], i + 1)
                wait_past(act, S["product"], i - 1)
                s.copy(k.tT[par][:, 0:KC, :], k.ps[0:128, 2, 0:2 * P]
                       .rearrange("f (c p) -> f c p", p=P)).then_inc(S["tT"], 1)

            def norm_c(i, par, half):
                act.wait_ge(S["nmr"], i + 1)
                s.activation(c2[par], c2[par], ACT.Identity, bias=k.st[par][:, 10:11],
                             scale=k.st[par][:, 9:10]).then_inc(S["y"], 1)

            def norm_x(i, par, half):
                act.wait_ge(S["nmr2"], i + 1)
                wait_past(act, S["turned2"], i - 1)
                s.activation(k.ho[par][:, :].unsqueeze(1), k.x3[:, bass.ds(i, 1), :], ACT.Relu, bias=k.st2[par][:, 10:11],
                             scale=k.st2[par][:, 9:10]).then_inc(S["h"], 1)

            def tT2_out(i, par, half):
                act.wait_ge(S["turned2"], i + 1)
                wait_past(act, S["product2"], i - 1)
                s.copy(k.tT[par][:, KC:2 * KC, :], k.ps[0:128, 4, 0:2 * P]
                       .rearrange("f (c p) -> f c p", p=P)).then_inc(S["tT2"], 1)

            def z_out(i, par, half):
                act.wait_ge(S["product2"], i + 1)
                if not isinstance(half, int) or half > 0:
                    act.wait_ge(stored[par], 32 * half)
                s.copy(k.z[par][:, :], k.ps[0:P, 5 + par, 0:ZW]).then_inc(S["z"], 1)

            pipelined(act, [(9, z_out), (8, tT2_out), (6, norm_x), (4, norm_c), (0, scale_high), (1, tT_out)])

        @block.vector
        def _(dve):
            v = nc.vector
            stt = v.scalar_tensor_tensor
            own, own2, own3 = Chain(dve, S["own"], 1), Chain(dve, S["own2"], 2), Chain(dve, S["own3"], 4)

            def combine(i, par, half):
                own.tile(i)
                dve.wait_ge(loaded[par], 16 * (half + 1))
                dve.wait_ge(S["aw"], i + 1)
                wait_past(dve, S["turned"], i - 1)
                wait_past(dve, S["t"], i)
                own.link(stt(out=k.sum[:, :], in0=k.hin[par][:, :], scalar=1.0 / CNT, in1=k.ps[0:P, par, FEAT:2 * FEAT],
                             op0=ALU.mult, op1=ALU.add))
                stt(out=k.t[par][:, :], in0=k.sum[:, :], scalar=k.dinvs[:, bass.ds(i, 1)], in1=k.aw[par][:, :],
                    op0=ALU.mult, op1=ALU.add).then_inc(S["t"], 1)

            def norm_c(i, par, half):
                own2.tile(i)
                st, c = k.st[par], c2[par]
                dve.wait_ge(S["product"], i + 1)
                wait_past(dve, S["x"], i - 1)
                v.tensor_tensor(c[:, :], k.ps[0:P, 3, 0:FEAT], k.bg[:, :], ALU.add).then_inc(S["u"], 1)
                dve.wait_ge(S["u"], i + 1)
                statistics(k, dve, own2, st, c[:, :], S["var"])

            def norm_x(i, par, half):
                own3.tile(i)
                st2, c = k.st2[par], c2[par]
                dve.wait_ge(S["y"], i + 1)
                own3.link(v.tensor_tensor(c[:, :], c[:, :], k.gamma[:, :], ALU.mult))
                own3.link(v.tensor_tensor(c[:, :], c[:, :], k.beta[:, :], ALU.add))
                dve.wait_ge(loaded_x[par], 16 * (half + 1))
                stt(out=k.x3[:, bass.ds(i, 1), :], in0=c[:, :].unsqueeze(1), scalar=0.0, in1=k.xin[par][:, :].unsqueeze(1),
                    op0=ALU.max, op1=ALU.add).then_inc(S["x"], 1)
                dve.wait_ge(S["x"], i + 1)
                settle(dve, k)
                statistics(k, dve, own3, st2, k.x3[:, bass.ds(i, 1), :].rearrange("p o f -> p (o f)"), S["var2"])

            pipelined(dve, [(5, norm_x), (3, norm_c), (0, combine)])


def attention(k):
    nc, d = k.nc, k.d
    PARTS, PT = 5, TILES // 5
    indexed, gathered, stored = k.sem("att_indexed"), [k.sem(f"att_gathered{n}") for n in range(PARTS)], k.sem("att_stored")
    shifted, raised, done, ok = (k.sem("att_" + n) for n in ("shifted", "raised", "done", "ok"))
    idx = k.st_i
    far = k.adj[:, :, :].rearrange("p t c -> p (t c)")[:, 0:4 * TILES * ZW].bitcast(F32).rearrange("p (t z) -> p t z", z=ZW)
    prod = k.adj[:, :, :].rearrange("p t c -> p (t c)")[:, 4 * TILES * ZW:4 * TILES * ZW + 4 * PT * FEAT].bitcast(F32)
    al = k.al
    with nc.Block() as block:

        @block.gpsimd
        def _(pool):
            pool.wait_ge(indexed, 32)
            for i in range(TILES):
                for out, table, side in ((al[:, i, :], d["alpha_l"], 0), (far[:, i, :], d["z"], 1)):
                    nc.gpsimd.indirect_dma_start(out, None, table[:, :], bass.IndirectOffsetOnAxis(ap=idx[:, side, i:i + 1], axis=0)
                                                 ).then_inc(gathered[i // PT], 16)

        @block.sync
        def _(sp):
            sp.dma_start(idx[:, 0, :], d["srcT"][:, 0:TILES]).then_inc(indexed, 16)
            sp.dma_start(idx[:, 1, :], d["dstT"][:, 0:TILES]).then_inc(indexed, 16)
            for n in range(PARTS):
                sp.wait_ge(done, n + 1)
                settle(sp, k)
                sp.dma_start(d["out"][n * PT * P:(n + 1) * PT * P, :].rearrange("(t p) f -> p t f", p=P),
                             k.x3[:, n * PT:(n + 1) * PT, :]).then_inc(stored, 16)
            sp.wait_ge(stored, 16 * PARTS)

        @block.scalar
        def _(act):
            for n in range(PARTS):
                act.wait_ge(shifted, n + 1)
                a = al[:, n * PT:(n + 1) * PT, :]
                nc.scalar.activation(a, a, ACT.Exp).then_inc(raised, 1)

        @block.vector
        def _(dve):
            v = nc.vector
            own = Chain(dve, ok, 100).tile(0)
            for n in range(PARTS):
                tiles = slice(n * PT, (n + 1) * PT)
                a, z, x = al[:, tiles, :], far[:, tiles, :], k.x3[:, tiles, :]
                most = k.st[0][:, 0:PT]
                dve.wait_ge(gathered[n], 32 * PT)
                own.link(v.tensor_tensor(a, a, z[:, :, FEAT:FEAT + HEADS], ALU.add))
                own.link(v.scalar_tensor_tensor(out=a, in0=a, scalar=0.01, in1=a, op0=ALU.mult, op1=ALU.max))
                own.link(v.tensor_reduce(most, a, AX.X, ALU.max))
                v.tensor_tensor(a, a, most.unsqueeze(2).to_broadcast([P, PT, HEADS]), ALU.subtract).then_inc(shifted, 1)
                dve.wait_ge(raised, n + 1)
                own.link(v.tensor_reduce(most, a, AX.X, ALU.add))
                own.link(v.reciprocal(most, most))
                own.link(v.tensor_tensor(a, a, most.unsqueeze(2).to_broadcast([P, PT, HEADS]), ALU.mult))
                own.link(v.tensor_tensor(prod.rearrange("p (t h c) -> p t h c", h=HEADS, c=DH),
                                         z[:, :, 0:FEAT].rearrange("p t (h c) -> p t h c", h=HEADS),
                                         a.unsqueeze(3).to_broadcast([P, PT, HEADS, DH]), ALU.mult))
                total = k.total[:, :].rearrange("p (t c) -> p t c", c=DH)
                own.link(v.tensor_reduce(total, prod.rearrange("p (t h c) -> p t c h", h=HEADS, c=DH), AX.X, ALU.add))
                v.tensor_tensor(x.rearrange("p t (h c) -> p t h c", h=HEADS), x.rearrange("p t (h c) -> p t h c", h=HEADS),
                                total.unsqueeze(2).to_broadcast([P, PT, HEADS, DH]), ALU.add).then_inc(done, 1)


def phases(k):
    d = k.d
    for phase in (
            setup, build, degrees,
            lambda k: edge_sums(k, "e0", d["h0"], "dstT", "srcT", UP / CNT),
            lambda k: mean_by_destination(k, "mean1", k.pairA, k.pairB, d["m1"], False),
            lambda k: edge_sums(k, "e1", d["m1"], "srcT", "dstT", 1.0 / CNT, True),
            lambda k: scatter_mean(k, "back1", k.pairB, True),
            lambda k: edge_sums(k, "e2", d["g"], "dstT", "srcT", 1.0 / CNT),
            lambda k: mean_by_destination(k, "mean2", k.pairA, k.pairB, d["m2"], True),
            lambda k: edge_sums(k, "e3", d["m2"], "srcT", "dstT", 1.0 / CNT),
            lambda k: scatter_mean(k, "back2", k.pairB, False),
            lambda k: edge_sums(k, "e4", d["h1"], "dstT", "srcT", UP / CNT),
            gru,
            lambda k: edge_sums(k, "e5", d["s2"], "dstT", "srcT", 1.0 / CNT),
            gcn, attention):
        phase(k)
        k.end_phase()


def program(nc, d):
    with ExitStack() as ctx:
        for name in ("h0", "m1", "g", "m2", "h1", "s2", "x1", "x2", "extra"):
            d[name] = nc.dram_tensor("t_" + name, (NODES, FEAT), F32).ap()
        d["adjT"] = nc.dram_tensor("t_adjT", (TILES, P, ROW // 4), U32).ap()
        d["z"] = nc.dram_tensor("t_z", (NODES, ZW), F32).ap()
        d["alpha_l"] = nc.dram_tensor("t_alpha_l", (NODES, HEADS), F32).ap()
        k = Kernel(nc, ctx, d)
        phases(k)


INPUTS = {"x": "x", "W1": "L0_gnn_W1", "b1": "L0_gnn_b1", "W2": "L0_gnn_W2", "b2": "L0_gnn_b2", "a": "L0_gnn_a",
          "relv": "L1_gnn_relvectors", "b_ih": "L1_gnn_b_ih", "b_hh": "L1_gnn_b_hh", "bg": "L2_gnn_b",
          "gamma": "L2_gnn_gamma", "beta": "L2_gnn_beta", "weight": "L3_gnn_weight"}


def kernel(**inputs):
    import concourse.bacc as _bacc
    import numpy as _np
    from concourse.bass_utils import run_bass_kernel_spmd as _run

    given = {name: _np.asarray(inputs[source]) for name, source in INPUTS.items()}
    for name, source in (("srcT", "src"), ("dstT", "dst"), ("relT", "edge_type_16")):
        given[name] = _np.asarray(inputs[source]).reshape(CHUNKS, P).T
    for name, source in (("w_ihT", "L1_gnn_w_ih"), ("w_hhT", "L1_gnn_w_hh"), ("WgT", "L2_gnn_W")):
        given[name] = _np.asarray(inputs[source]).T
    for name, source in (("attn_l", "L3_gnn_attn_l"), ("attn_r", "L3_gnn_attn_r")):
        given[name] = _np.asarray(inputs[source]).reshape(FEAT)
    nc = _bacc.Bacc("TRN2", target_bir_lowering=False, num_devices=1)
    arrays, d = {}, {}
    for name, a in given.items():
        arrays["in_" + name] = _np.ascontiguousarray(a)
        d[name] = nc.dram_tensor("in_" + name, a.shape, mybir.dt.from_np(a.dtype), kind="ExternalInput").ap()
    d["out"] = nc.dram_tensor("out", (NODES, FEAT), F32, kind="ExternalOutput").ap()
    program(nc, d)
    r = _run(nc, [arrays], core_ids=[0])
    return r.results[0]["out"]
```
